# Optimizing a Trainium2 kernel written in Bass

```python
import numpy as np
import jax
import jax.numpy as jnp

def _softmax(x, axis=-1):
    return jax.nn.softmax(x, axis=axis)

def _gelu(x):
    return jax.nn.gelu(x, approximate=True)

def _silu(x):
    return jax.nn.silu(x)

def _sigmoid(x):
    return jax.nn.sigmoid(x)

def _layernorm(x, axis=-1, eps=1e-05):
    m = jnp.mean(x, axis=axis, keepdims=True)
    v = jnp.var(x, axis=axis, keepdims=True)
    return (x - m) / jnp.sqrt(v + eps)

def _scatter_add(tgt, idx, src, axis=0):
    return tgt.at[idx].add(src)

def _segment_sum(src, seg, n):
    return jax.ops.segment_sum(src, seg, n)
kernel_name = 'mk_seq_postln_d1_jaxref_r8_1c47c1'

def setup_inputs(seed: int=0):
    np.random.seed(seed)
    _w = jnp.asarray

    def _L0_attn_setup():
        import jax, jax.numpy as jnp
        import numpy as np
        NUM_HEADS = 16
        WINDOW_SIZE = 32
        key = jax.random.key(seed)
        ks = jax.random.split(key, 5)
        B, S, H = (2, 256, 128)
        scale = 0.02
        return {'x': jax.random.normal(ks[0], (B, S, H), dtype=jnp.float32), 'Wq': jax.random.normal(ks[1], (H, H), dtype=jnp.float32) * scale, 'bq': jnp.zeros((H,), dtype=jnp.float32), 'Wk': jax.random.normal(ks[2], (H, H), dtype=jnp.float32) * scale, 'bk': jnp.zeros((H,), dtype=jnp.float32), 'Wv': jax.random.normal(ks[3], (H, H), dtype=jnp.float32) * scale, 'bv': jnp.zeros((H,), dtype=jnp.float32), 'Wo': jax.random.normal(ks[4], (H, H), dtype=jnp.float32) * scale, 'bo': jnp.zeros((H,), dtype=jnp.float32)}
    _L0_attn_in = _L0_attn_setup()

    def _L0_ffn_setup():
        import jax, jax.numpy as jnp
        import numpy as np
        D = 128
        H = 512
        E = 8
        TOPK = 2
        CAP_F = 1.25
        key = jax.random.key(seed)
        ks = jax.random.split(key, 6)
        sc = 0.02
        return {'x': jax.random.normal(ks[0], (4, 256, D), jnp.float32), 'Wg': jax.random.normal(ks[1], (D, E), jnp.float32) * sc, 'bg': jnp.zeros((E,), jnp.float32), 'W1': jax.random.normal(ks[2], (E, D, H), jnp.float32) * sc, 'W2': jax.random.normal(ks[3], (E, D, H), jnp.float32) * sc, 'W3': jax.random.normal(ks[4], (E, H, D), jnp.float32) * sc}
    _L0_ffn_in = _L0_ffn_setup()
    _d = {'L0_attn_x': _L0_attn_in['x'], 'L0_attn_Wq': _L0_attn_in['Wq'], 'L0_attn_bq': _L0_attn_in['bq'], 'L0_attn_Wk': _L0_attn_in['Wk'], 'L0_attn_bk': _L0_attn_in['bk'], 'L0_attn_Wv': _L0_attn_in['Wv'], 'L0_attn_bv': _L0_attn_in['bv'], 'L0_attn_Wo': _L0_attn_in['Wo'], 'L0_attn_bo': _L0_attn_in['bo'], 'L0_ffn_Wg': _L0_ffn_in['Wg'], 'L0_ffn_bg': _L0_ffn_in['bg'], 'L0_ffn_W1': _L0_ffn_in['W1'], 'L0_ffn_W2': _L0_ffn_in['W2'], 'L0_ffn_W3': _L0_ffn_in['W3']}
    _x0 = _d['L0_attn_x']
    _d['L0_attn_x'] = jax.random.normal(jax.random.fold_in(jax.random.key(seed), 1), (4, 512, 128), dtype=_x0.dtype)
    del _x0
    return _d

def reference(L0_attn_x, L0_attn_Wq, L0_attn_bq, L0_attn_Wk, L0_attn_bk, L0_attn_Wv, L0_attn_bv, L0_attn_Wo, L0_attn_bo, L0_ffn_Wg, L0_ffn_bg, L0_ffn_W1, L0_ffn_W2, L0_ffn_W3):

    def _L0_attn_ref(x, Wq, bq, Wk, bk, Wv, bv, Wo, bo):
        import jax, jax.numpy as jnp
        import numpy as np
        NUM_HEADS = 16
        WINDOW_SIZE = 32
        B, S, Hs = x.shape
        nh = NUM_HEADS
        hd = Hs // nh
        half_w = WINDOW_SIZE // 2
        q = (x @ Wq + bq).reshape(B, S, nh, hd)
        k = (x @ Wk + bk).reshape(B, S, nh, hd)
        v = (x @ Wv + bv).reshape(B, S, nh, hd)
        scores = jnp.einsum('bqhd,bkhd->bhqk', q, k) / jnp.sqrt(jnp.asarray(hd, x.dtype))
        idx = jnp.arange(S)
        band = jnp.abs(idx[:, None] - idx[None, :]) <= half_w
        scores = jnp.where(band[None, None, :, :], scores, -jnp.inf)
        attn = jax.nn.softmax(scores, axis=-1)
        out = jnp.einsum('bhqk,bkhd->bqhd', attn, v).reshape(B, S, Hs)
        return out @ Wo + bo

    def _L0_ffn_ref(x, Wg, bg, W1, W2, W3):
        import jax, jax.numpy as jnp
        import numpy as np
        D = 128
        H = 512
        E = 8
        TOPK = 2
        CAP_F = 1.25
        b, s, d = x.shape
        xt = x.reshape(-1, d)
        T = xt.shape[0]
        capacity = int(T / E * CAP_F)
        gate_logits = xt @ Wg + bg
        top_v, top_i = jax.lax.top_k(gate_logits, TOPK)
        expert_label = jax.nn.one_hot(top_i, E, dtype=xt.dtype).sum(axis=1)
        seq = jnp.cumsum(expert_label, axis=0) * expert_label
        valid = (seq > 0) & (seq <= capacity)
        slot = (seq - 1.0).astype(jnp.int32)
        flat_idx = jnp.where(valid, jnp.arange(E, dtype=jnp.int32)[None, :] * capacity + slot, E * capacity)
        src = jnp.broadcast_to(xt[:, None, :], (T, E, d)).reshape(-1, d)
        buf = jnp.zeros((E * capacity + 1, d), xt.dtype).at[flat_idx.reshape(-1)].set(src)
        disp = buf[:-1].reshape(E, capacity, d)
        h = jax.nn.silu(jnp.einsum('ecd,edh->ech', disp, W1)) * jnp.einsum('ecd,edh->ech', disp, W2)
        out = jnp.einsum('ech,ehd->ecd', h, W3)
        out_flat = jnp.concatenate([out.reshape(E * capacity, d), jnp.zeros((1, d), xt.dtype)], axis=0)
        all_expert_output = out_flat[flat_idx]
        sel = jnp.take_along_axis(all_expert_output, top_i[:, :, None], axis=1)
        routing_w = jax.nn.softmax(top_v, axis=-1)
        y = (routing_w[:, :, None] * sel).sum(axis=1)
        return y.reshape(b, s, d)
    x = L0_attn_x
    x = _layernorm(x + _L0_attn_ref(x, L0_attn_Wq, L0_attn_bq, L0_attn_Wk, L0_attn_bk, L0_attn_Wv, L0_attn_bv, L0_attn_Wo, L0_attn_bo), axis=-1)
    x = _layernorm(x + _L0_ffn_ref(x, L0_ffn_Wg, L0_ffn_bg, L0_ffn_W1, L0_ffn_W2, L0_ffn_W3), axis=-1)
    return x

_drawn_inputs = setup_inputs


def setup_inputs(seed=0):
    import zlib

    import numpy as np

    out = dict(_drawn_inputs(seed))
    spreads = {'L0_attn_bq': (0.0, 0.8),
     'L0_attn_bk': (0.0, 0.8),
     'L0_attn_bv': (0.0, 0.379),
     'L0_attn_bo': (0.0, 0.1),
     'L0_ffn_bg': (0.0, 0.8)}
    factors = {'L0_attn_Wq': 8.0,
     'L0_attn_Wk': 8.0,
     'L0_attn_Wv': 6.36,
     'L0_ffn_Wg': 8.0,
     'L0_ffn_W1': 8.0,
     'L0_ffn_W2': 8.0,
     'L0_ffn_W3': 8.0}
    for name, (base, spread) in spreads.items():
        noise = np.random.default_rng([zlib.crc32(name.encode()), seed]).standard_normal(out[name].shape)
        drawn = base * np.exp(spread * noise) if base else spread * noise
        out[name] = jnp.asarray(drawn.astype(out[name].dtype))
    for name, factor in factors.items():
        out[name] = (out[name] * factor).astype(out[name].dtype)
    return out
```

```python
from contextlib import ExitStack

import numpy as np

import concourse.bass as bass
from concourse import mybir

ALU = mybir.AluOpType
ACT = mybir.ActivationFunctionType
AX = mybir.AxisListType.X
F32 = mybir.dt.float32
F32R = mybir.dt.float32r
FP16 = mybir.dt.float16
BF16 = mybir.dt.bfloat16
I32 = mybir.dt.int32

P = 128
B, S, D = 4, 512, 128
T = B * S
NT = T // P
NH, HD = 16, 8
HG, NG = 4, 4
HALF = 16
QB, KW = 32, 64
UB = 8
UT = UB * QB
NU = T // UT
PAIRS = [(0, 2), (1, 3), (4, 6), (5, 7)]
SP = S + 2 * HALF
NTERM = 3
KR = NTERM * HG * HD
OC = 2 * HG * HD + 2
E, H, CAP = 8, 512, 320
HC = H // P
ROW = D + 2
TR = S // P
ROUNDS = NU + 3
BIG = -1.0e30
SCALE = float(HD) ** -0.5
EPS = 1e-5


def constants():
    def bf16(a):
        return (np.ascontiguousarray(a, dtype=np.float32).view(np.uint32) >> 16).astype(np.uint16)

    p = np.arange(P)
    c = {}
    c["c_ident"] = np.eye(P, dtype=np.float32)
    c["c_identb"] = bf16(np.eye(P))
    j, k = np.arange(QB)[:, None, None], np.arange(KW)[None, None, :]
    b = np.arange(S // QB)[None, :, None]
    key = QB * b - HALF + k
    seen = (k >= j) & (k <= j + 2 * HALF) & (key >= 0) & (key < S)
    mask = np.where(seen, 0.0, BIG)
    c["c_mask"] = bf16(mask)
    c["c_onehot"] = bf16(p[None, :] % QB == np.arange(QB)[:, None])
    aux = np.zeros((96, 2, 4, NG, P), np.float32)
    for half in range(2):
        for i, pair in enumerate(PAIRS):
            for g in range(NG):
                for s, blk in enumerate(pair):
                    cols = slice(KW * s, KW * s + KW)
                    aux[blk * NG + g, half, i, g, cols] = 1
                    aux[32 + blk * NG + g, half, i, g, cols] = 1
                    aux[64:96, half, i, g, cols] = mask[:, half * UB + blk, :]
    c["c_aux"] = bf16(aux.reshape(96, -1))
    c["c_tri"] = bf16(p[:, None] <= p[None, :])
    c["c_merge"] = (p[:, None] % QB == np.arange(QB)[None, :]).astype(np.float16)
    vx = np.zeros((P, 4 * NG, OC), np.float16)
    vx[:KW, :, 64] = 1
    vx[KW:, :, 65] = 1
    c["c_vx"] = vx.reshape(P, -1)
    f = np.zeros((P, 64), np.float32)
    f[:, 0:4] = p[:, None] // QB == np.arange(HG)
    f[:, 4:8] = (p[:, None] % 32) // HD == np.arange(HG)
    f[:, 8:16] = E - np.arange(E)
    f[:, 16:32] = T * 0 + p[:, None] + P * np.arange(NT)
    c["c_small"] = f
    d = np.zeros((E * CAP, ROW), np.float32)
    d[:, D + 1] = 2 * T + np.arange(E * CAP)
    c["c_disp"] = d
    return c


def layer_kernel(nc, x, Wq, bq, Wk, bk, Wv, bv, Wo, bo, Wg, bg, W1, W2, W3,
                 c_ident, c_identb, c_mask, c_onehot, c_aux, c_tri, c_merge, c_vx, c_small, c_disp, out):
    c_identb, c_mask, c_onehot, c_aux, c_tri = (a.bitcast(BF16) for a in (c_identb, c_mask, c_onehot, c_aux, c_tri))
    x_d = x.rearrange("b (t p) d -> b p t d", p=P)
    out_d = out.rearrange("b (t p) d -> b p t d", p=P)
    disp = nc.dram_tensor("dispatched", [E * CAP + 2 * T, ROW], F32).ap()
    back = nc.dram_tensor("returned", [2 * T + E * CAP, D], F32).ap()

    order = []
    for u in range(ROUNDS):
        if u < NU:
            if u % 2 == 0:
                order += [("xT", u // 2), ("q", u // 2), ("k", u // 2)]
            order += [("V", u)]
        for j in range(4):
            order += [use for use in after_step(u, j) if use[0] in PSUM_USES]
        if u < NU:
            order += [("mT", u)]
    spare = {use: n for n, use in enumerate(order)}

    with ExitStack() as ctx:
        def sem(name):
            return ctx.enter_context(nc.semaphore(name))

        def sb(name, shape, dt, c=ctx):
            return c.enter_context(nc.sbuf_tensor(name, shape, dt))

        def ps(name, dt=F32):
            return ctx.enter_context(nc.psum_tensor(name, [P, 512], dt))

        w_hi = sb("w_hi", [P, E, 3 * H], F32R)
        w_lo = sb("w_lo", [P, E, 3 * H], F32R)
        w_raw = sb("w_raw", [P, 3, H], F32)
        x2a = sb("x2a", [P, NT, ROW], F32)
        x2b = sb("x2b", [P, TR, ROW], F32)
        ident = sb("ident", [P, P], F32)
        small = sb("small", [P, 64], F32)
        stats = sb("stats", [P, 4, 6], F32)
        mv = sb("mv", [P, 4, 2], F32)
        vareps = sb("vareps", [P, 4], F32)
        rstd = sb("rstd", [P, 4], F32)
        mhalf = sb("mhalf", [P, 4], F32)

        actx = ExitStack()
        x_sb = sb("x_sb", [P, NT, D], F32, actx)
        xT_hi = sb("xT_hi", [P, 2, SP], FP16, actx)
        xT_lo = sb("xT_lo", [P, 2, SP], FP16, actx)
        wp_hi = sb("wp_hi", [P, 4, D], FP16, actx)
        wp_lo = sb("wp_lo", [P, 4, D], FP16, actx)
        qk_hi = sb("qk_hi", [P, 2, S], FP16, actx)
        qk_lo = sb("qk_lo", [P, 2, S], FP16, actx)
        q3 = sb("q3", [KR, NG, S], FP16, actx)
        k3 = sb("k3", [KR, 2, NG, SP], FP16, actx)
        qx = sb("qx", [KR, 2, NG, UB, HG * QB], FP16, actx)
        vx_hi = sb("vx_hi", [P, 2, 4 * NG, OC], FP16, actx)
        vx_lo = sb("vx_lo", [P, 2, 4 * NG, OC], FP16, actx)
        p32 = sb("p32", [P, 2, 512], F32, actx)
        p_hi = sb("p_hi", [P, 2, 512], FP16, actx)
        p_lo = sb("p_lo", [P, 2, 512], FP16, actx)
        o32 = sb("o32", [P, 2, NG * 64], F32, actx)
        o_hi = sb("o_hi", [P, 4, 2, P], FP16, actx)
        o_lo = sb("o_lo", [P, 4, 2, P], FP16, actx)
        rden = sb("rden", [P, NG, 2], F32, actx)
        rmask = sb("rmask", [P, NG, 2, HG], F32, actx)
        nmax = sb("nmax", [P, 2, UB * NG], F32, actx)
        nmax2 = sb("nmax2", [P, 2, UB * NG], BF16, actx)
        mT = sb("mT", [96, 2, P], BF16, actx)
        at_hi = sb("at_hi", [P, UT], FP16, actx)
        at_lo = sb("at_lo", [P, UT], FP16, actx)
        res = sb("res", [P, 2, D], F32, actx)
        x2T = sb("x2T", [P, S], F32, actx)
        identb = sb("identb", [P, P], BF16, actx)
        mask = sb("mask", [QB, S // QB, KW], BF16, actx)
        onehot = sb("onehot", [QB, P], BF16, actx)
        aux = sb("aux", [96, 2, 4, NG, P], BF16, actx)
        tri = sb("tri", [P, P], BF16, actx)
        ones = sb("ones", [P, P], BF16, actx)
        merge = sb("merge", [P, QB], FP16, actx)
        bias = sb("bias", [P, 4], F32, actx)
        bo_row = sb("bo_row", [P, D], F32, actx)
        bg_row = sb("bg_row", [P, E], F32, actx)
        wg = sb("wg", [P, E], F32, actx)
        lg = sb("lg", [P, TR, E], F32, actx)
        tmp = sb("tmp", [P, TR, E], F32, actx)
        pick = sb("pick", [P, 2, TR, E], F32, actx)
        top = sb("top", [P, 2, TR], F32, actx)
        pos = sb("pos", [P, 2, TR], F32, actx)
        label = sb("label", [P, TR, E], BF16, actx)
        seq = sb("seq", [P, TR, E], F32, actx)
        base = sb("base", [P, E], F32, actx)
        slot = sb("slot", [P, 2, TR], F32, actx)
        flat = sb("flat", [P, 2, TR], F32, actx)
        valid = sb("valid", [P, 2, TR], F32, actx)
        gap = sb("gap", [P, TR], F32, actx)
        egap = sb("egap", [P, TR], F32, actx)
        wgt = sb("wgt", [P, 2, TR], F32, actx)
        index = sb("index", [P, 2, TR], I32, actx)
        zero = sb("zero", [P, 1024], F32, actx)
        actx.close()

        ectx = ExitStack()
        xe = sb("xe", [P, 3, 3, ROW], F32, ectx)
        xeT_hi = sb("xeT_hi", [P, 2, CAP], F32R, ectx)
        xeT_lo = sb("xeT_lo", [P, 2, CAP], F32R, ectx)
        gate = sb("gate", [P, 2, CAP], F32, ectx)
        h32 = sb("h32", [P, 2, CAP], F32, ectx)
        h_hi = sb("h_hi", [P, 4, CAP], F32R, ectx)
        h_lo = sb("h_lo", [P, 4, CAP], F32R, ectx)
        yT = sb("yT", [P, 2, CAP], F32, ectx)
        ye = sb("ye", [P, 2, 3, D], F32, ectx)
        ret = sb("ret", [P, 3, 3], I32, ectx)
        y01 = sb("y01", [P, 2, 2, TR, D], F32, ectx)
        z = sb("z", [P, 2, TR, D], F32, ectx)
        zo = sb("zo", [P, 2, TR, D], F32, ectx)
        ectx.close()

        s_bank = [ps("s_bank0"), ps("s_bank1")]
        t_bank = [ps("t_bank0"), ps("t_bank1")]
        o_bank = [ps("o_bank0"), ps("o_bank1")]
        m_bank = [ps("m_bank0"), ps("m_bank1")]

        def mb(use):
            return m_bank[spare[use] % 2]

        def count(*use):
            return spare[use] + 1

        x_in = [sem(f"x_in{b}") for b in range(B)]
        wp_in, consts_in, tables_in, wg_in, mT_rows_in = map(sem, ("wp_in", "consts_in", "tables_in", "wg_in", "mT_rows_in"))
        zeroed, dram_set = sem("zeroed"), sem("dram_set")
        wp_split_hi, wp_split = sem("wp_split_hi"), sem("wp_split")
        spare_filled, spare_free = sem("spare_filled"), sem("spare_free")
        xT_hi_done = sem("xT_hi_done")
        qk_hi_done = sem("qk_hi_done")
        q3_in, k3_in = sem("q3_in"), sem("k3_in")
        qx_done = sem("qx_done")
        vx_hi_done = sem("vx_hi_done")
        s_filled, s_maxed = sem("s_filled"), sem("s_maxed")
        nmax_hi, nmax_split = sem("nmax_hi"), sem("nmax_split")
        t_filled, p32_done, p_hi_done, p_lo_done = map(sem, ("t_filled", "p32_done", "p_hi_done", "p_lo_done"))
        o_filled, o32_done, o_hi_done, o_lo_done = map(sem, ("o_filled", "o32_done", "o_hi_done", "o_lo_done"))
        at_hi_done = sem("at_hi_done")
        bo_added = sem("bo_added")
        var_done, rstd_done, x2_done, x2b_done = map(sem, ("var_done", "rstd_done", "x2_done", "x2b_done"))
        gap_done, egap_done, label_done = map(sem, ("gap_done", "egap_done", "label_done"))
        rows_done, sent = sem("rows_done"), [sem(f"sent{i}") for i in range(2)]
        w_in = [sem(f"w_in{i}") for i in range(3)]
        w_hi_done, w_split = sem("w_hi_done"), sem("w_split")
        xe_in = [sem(f"xe_in{i}") for i in range(3)]
        xeT_filled, xeT_hi_done, xeT_split = map(sem, ("xeT_filled", "xeT_hi_done", "xeT_split"))
        ab_filled, gate_done, h_done, h_hi_done, h_split = map(sem, ("ab_filled", "gate_done", "h_done", "h_hi_done", "h_split"))
        w3_done, yT_done, yb_filled, ye_done, ret_done = map(sem, ("w3_done", "yT_done", "yb_filled", "ye_done", "ret_done"))
        returned = [sem("returned_even"), sem("returned_odd")]
        y_in = [sem("y_in0"), sem("y_in1")]
        fin_var, fin_rstd, fin_done = sem("fin_var"), sem("fin_rstd"), sem("fin_done")
        stored = [sem("stored_even"), sem("stored_odd")]
        chain = sem("vector_chain")

        block = ctx.enter_context(nc.Block())

        @block.sync
        def _(sp):
            sp.dma_start(x_sb[:, 0:TR, :], x_d[0]).then_inc(x_in[0], 16)
            for i, w in enumerate((Wq, Wk, Wv, Wo)):
                sp.dma_start(p32[:, 0, i * D:(i + 1) * D], w).then_inc(wp_in, 16)
            for t, src in ((ident[:], c_ident), (small[:], c_small), (identb[:], c_identb),
                           (vx_hi[:, 0].rearrange("p a c -> p (a c)"), c_vx),
                           (vx_hi[:, 1].rearrange("p a c -> p (a c)"), c_vx),
                           (mask[:], c_mask), (onehot[:], c_onehot),
                           (merge[:], c_merge), (tri[:], c_tri),
                           (bias[:, 0:1], bq.rearrange("(a b) -> a b", b=1)),
                           (bias[:, 1:2], bk.rearrange("(a b) -> a b", b=1)),
                           (bias[:, 2:3], bv.rearrange("(a b) -> a b", b=1))):
                sp.dma_start(t, src).then_inc(consts_in, 16)
            for i in range(2):
                sp.dma_start(mT[64:96, i, :], c_onehot).then_inc(mT_rows_in, 16)
            sp.dma_start(aux[:].rearrange("p a b c d -> p (a b c d)"), c_aux).then_inc(tables_in, 16)
            sp.dma_start(wg[:], Wg).then_inc(tables_in, 16)
            sp.dma_start(bo_row[:], bo.partition_broadcast(P)).then_inc(tables_in, 16)
            sp.dma_start(bg_row[:], bg.partition_broadcast(P)).then_inc(tables_in, 16)
            for b in range(1, B):
                sp.dma_start(x_sb[:, b * TR:(b + 1) * TR, :], x_d[b]).then_inc(x_in[b], 16)

            def w_load(n):
                e, part = divmod(n, 3)
                if n >= 3:
                    sp.wait_ge(w_split, n - 2)
                dst, src = w_raw[:, n % 3, :], (W1, W2, W3)[part][e]
                if part == 2:
                    dst, src = dst.rearrange("p (c d) -> p c d", c=HC), src.rearrange("(c p) d -> p c d", p=P)
                sp.dma_start(dst, src).then_inc(w_in[part], 16)

            for u in range(NU):
                if u % 2 == 0:
                    b = u // 2
                    for i, dst in enumerate((q3, k3)):
                        sp.wait_ge(spare_free, count("qk"[i], b))
                        if i == 0 and b >= 1:
                            sp.wait_ge(qx_done, HG * 2 * b)
                        if i == 1 and b >= 2:
                            sp.wait_ge(s_filled, 8 * (b - 1))
                            sp.wait_ge(t_filled, 8 * (b - 1))
                        for g in range(NG):
                            rows = slice(32 * g, 32 * g + 32)
                            for term in range(NTERM):
                                part = qk_lo if term == 1 + i else qk_hi
                                to = (q3[32 * term:32 * term + 32, g, :] if i == 0 else
                                      k3[32 * term:32 * term + 32, b % 2, g, HALF:HALF + S])
                                sp.dma_start(to, part[rows, i, :]).then_inc((q3_in, k3_in)[i], 16)
                if u == 0:
                    sp.dma_start(disp[0:E * CAP, :], c_disp).then_inc(dram_set, 16)
                    sp.wait_ge(zeroed, 1)
                    for i in range(2 * T * D // (P * 1024)):
                        rows = 1024 * P // D
                        sp.dma_start(back[i * rows:(i + 1) * rows, :].rearrange("(p r) d -> p (r d)", p=P),
                                     zero[:]).then_inc(dram_set, 16)
                for i in range(3):
                    w_load(3 * u + i)

            for e in range(E):
                if e == 0:
                    for i in range(2):
                        sp.wait_ge(sent[i], 16 * TR * 2 * 2)
                if e >= 3:
                    sp.wait_ge(ye_done, 3 * (e - 2))
                    sp.wait_ge(ret_done, 2 * (e - 2))
                rows = disp[e * CAP:(e + 1) * CAP, :]
                sp.dma_start(xe[:, e % 3, 0:2, :], rows[0:256, :].rearrange("(j p) d -> p j d", p=P)).then_inc(xe_in[e % 3], 16)
                sp.dma_start(xe[0:64, e % 3, 2, :], rows[256:CAP, :]).then_inc(xe_in[e % 3], 16)
            for i in range(2):
                sp.wait_ge(returned[i], 48 * E // 2)
            for b in range(B):
                if b >= 2:
                    sp.wait_ge(fin_done, TR * (b - 1))
                for i in range(2):
                    src = back[i * T + b * S:i * T + (b + 1) * S, :].rearrange("(t p) d -> p t d", p=P)
                    sp.dma_start(y01[:, b % 2, i], src).then_inc(y_in[b % 2], 16)
            for i in range(2):
                sp.wait_ge(stored[i], 16 * B // 2)

        @block.gpsimd
        def _(gp):
            gp.memset(zero[:], 0.0).then_inc(zeroed, 1)
            gp.memset(mhalf[:], -0.5).then_inc(zeroed, 1)
            gp.memset(ones[:], 1.0).then_inc(zeroed, 1)
            gp.memset(base[:], 0.0).then_inc(zeroed, 1)
            for t in (xT_hi, xT_lo):
                for i in range(2):
                    gp.memset(t[:, i, 0:HALF], 0.0).then_inc(zeroed, 1)
                    gp.memset(t[:, i, HALF + S:SP], 0.0).then_inc(zeroed, 1)
            for i in range(2):
                gp.memset(k3[:, i, :, 0:HALF], 0.0).then_inc(zeroed, 1)
                gp.memset(k3[:, i, :, HALF + S:SP], 0.0).then_inc(zeroed, 1)
            gp.memset(vx_lo[:], 0.0).then_inc(zeroed, 1)

            def w_split_third(n):
                e, part = divmod(n, 3)
                gp.wait_ge(w_in[part], 16 * (e + 1))
                cols = slice(part * H, (part + 1) * H)
                gp.tensor_copy(w_hi[:, e, cols], w_raw[:, n % 3, :]).then_inc(w_hi_done, 1)
                gp.wait_ge(w_hi_done, n + 1)
                gp.tensor_tensor(w_lo[:, e, cols], w_raw[:, n % 3, :], w_hi[:, e, cols].bitcast(F32),
                                 ALU.subtract).then_inc(w_split, 1)

            def o_low(n):
                j = n % 4
                gp.wait_ge(o_hi_done, n + 1)
                gp.tensor_tensor(o_lo[:, j].rearrange("p s (g c) -> p s g c", g=NG),
                                 o32[:, n % 2, :].rearrange("p (g s c) -> p s g c", g=NG, s=2),
                                 o_hi[:, j].rearrange("p s (g c) -> p s g c", g=NG),
                                 ALU.subtract).then_inc(o_lo_done, 1)

            for u in range(ROUNDS):
                if u < NU:
                    if u == 0:
                        gp.wait_ge(consts_in, 16 * 12)
                    gp.wait_ge(q3_in, 16 * 12 * (u // 2 + 1))
                    if u >= 2:
                        gp.wait_ge(t_filled, 4 * (u - 1))
                    src = q3[:, :, (u % 2) * UT:(u % 2 + 1) * UT].rearrange("p g (b q) -> p g b q", b=UB)
                    for h in range(HG):
                        gp.tensor_scalar(qx[:, u % 2, :, :, h * QB:(h + 1) * QB], src, small[0:KR, 4 + h:5 + h],
                                         1.0, ALU.mult, ALU.mult).then_inc(qx_done, 1)
                if u == 0:
                    gp.wait_ge(tables_in, 16 * 4)
                if u < NU and u % 2 == 0:
                    b = u // 2
                    gp.wait_ge(spare_filled, count("xT", b))
                    xb = x_sb[:, b * TR:(b + 1) * TR, :]
                    gp.tensor_tensor(xb, xb, bo_row[:].unsqueeze(1).to_broadcast([P, TR, D]), ALU.add).then_inc(bo_added, 1)
                for j in range(4):
                    if 1 <= u <= NU and j < 3:
                        w_split_third(3 * (u - 1) + j)
                    if 1 <= u <= NU and j >= 1:
                        o_low(4 * (u - 1) + j - 1)
                    for what, i in after_step(u, j):
                        if what == "WO":
                            gp.wait_ge(var_done, i + 1)
                            gp.tensor_tensor(rstd[:, 0:2], vareps[:, 0:2], mhalf[:, 0:2], ALU.pow).then_inc(rstd_done, 1)
                        if what == "RK":
                            if i == 0:
                                gp.wait_ge(dram_set, 16 * 5)
                            gp.wait_ge(rows_done, i + 1)
                            for t in range(TR):
                                for k in range(2):
                                    rows = x2a[:, i * TR + t, :] if k == 0 else x2b[:, t, :]
                                    gp.indirect_dma_start(
                                        disp, bass.IndirectOffsetOnAxis(ap=index[:, k, t:t + 1], axis=0),
                                        rows, None).then_inc(sent[i % 2], 16)
                if 1 <= u <= NU:
                    o_low(4 * (u - 1) + 3)

            for e in range(E):
                gp.wait_ge(ye_done, 3 * (e + 1))
                gp.wait_ge(ret_done, 2 * (e + 1))
                for j in range(3):
                    n = P if j < 2 else 64
                    gp.indirect_dma_start(
                        back, bass.IndirectOffsetOnAxis(ap=ret[0:n, e % 3, j:j + 1], axis=0),
                        ye[0:n, e % 2, j, :], None).then_inc(returned[e % 2], 16)
            for b in range(B):
                gp.wait_ge(fin_var, b + 1)
                gp.tensor_tensor(rstd[:], vareps[:], mhalf[:], ALU.pow).then_inc(fin_rstd, 1)

        @block.scalar
        def _(act):
            def o_high(n):
                act.wait_ge(o32_done, n + 1)
                if n % 4 == 0 and n >= 4:
                    act.wait_ge(spare_filled, count("AT", n // 4 - 1))
                act.activation(o_hi[:, n % 4].rearrange("p s (g c) -> p s g c", g=NG),
                               o32[:, n % 2, :].rearrange("p (g s c) -> p s g c", g=NG, s=2), ACT.Copy).then_inc(o_hi_done, 1)

            act.wait_ge(wp_in, 64)
            act.activation(wp_hi[:].rearrange("p a b -> p (a b)"), p32[:, 0, :], ACT.Copy).then_inc(wp_split_hi, 1)
            act.wait_ge(consts_in, 16 * 12)
            act.wait_ge(zeroed, 17)
            for u in range(ROUNDS):
                if u < NU:
                    if u % 2 == 0:
                        b = u // 2
                        act.wait_ge(spare_filled, count("xT", b))
                        act.activation(xT_hi[:, b % 2, HALF:HALF + S], mb(("xT", b))[:, :], ACT.Copy).then_inc(xT_hi_done, 1)
                        for i, what in enumerate("qk"):
                            act.wait_ge(spare_filled, count(what, b))
                            if b >= 1:
                                act.wait_ge((q3_in, k3_in)[i], 16 * 12 * b)
                            act.activation(qk_hi[:, i, :], mb((what, b))[:, :], ACT.Identity,
                                           bias=bias[:, i:i + 1]).then_inc(qk_hi_done, 1)
                    act.wait_ge(spare_filled, count("V", u))
                    v = mb(("V", u))[:, :].rearrange("p (a c) -> p a c", c=32)
                    act.activation(vx_hi[0:64, u % 2, :, 0:32], v[0:64], ACT.Copy).then_inc(vx_hi_done, 1)
                    act.activation(vx_hi[64:128, u % 2, :, 32:64], v[64:128], ACT.Copy).then_inc(vx_hi_done, 1)
                for j in range(4):
                    if 1 <= u <= NU:
                        n = 4 * (u - 1) + j
                        act.wait_ge(t_filled, n + 1)
                        if n >= 2:
                            act.wait_ge(p_lo_done, n - 1)
                            act.wait_ge(o_filled, n - 1)
                        if n == 0:
                            act.wait_ge(wp_split, 1)
                        act.activation(p32[:, n % 2, :], t_bank[n % 2][:, :], ACT.Exp, scale=SCALE).then_inc(p32_done, 1)
                        act.activation(p_hi[:, n % 2, :], t_bank[n % 2][:, :], ACT.Exp, scale=SCALE).then_inc(p_hi_done, 1)
                        if j >= 1:
                            o_high(n - 1)
                    for what, i in after_step(u, j):
                        if what == "AT":
                            act.wait_ge(spare_filled, count(what, i))
                            act.activation(at_hi[:], mb((what, i))[:, 0:UT], ACT.Identity, bias=bias[:, 2:3]).then_inc(at_hi_done, 1)
                        if what == "copy":
                            act.wait_ge(x2_done, 4 * i + 4)
                            if i >= 1:
                                act.wait_ge(sent[(i - 1) % 2], 16 * TR * 2 * ((i - 1) // 2 + 1))
                            act.activation(x2b[:, :, 0:D], x2a[:, i * TR:(i + 1) * TR, 0:D], ACT.Copy).then_inc(x2b_done, 1)
                        if what == "LG":
                            act.wait_ge(gap_done, i + 1)
                            act.activation(egap[:], gap[:], ACT.Exp).then_inc(egap_done, 1)
                if 1 <= u <= NU:
                    o_high(4 * (u - 1) + 3)

            def expert_in(e):
                act.wait_ge(xeT_filled, e + 1)
                act.activation(xeT_hi[:, e % 2, :], m_bank[0][:, 0:CAP], ACT.Copy).then_inc(xeT_hi_done, 1)

            def expert_out(e):
                act.wait_ge(w3_done, HC * (e + 1))
                if e >= 2:
                    act.wait_ge(yb_filled, e - 1)
                act.activation(yT[:, e % 2, :], o_bank[e % 2][:, 0:CAP], ACT.Copy).then_inc(yT_done, 1)

            expert_in(0)
            for m in range(HC * E + 4):
                if m < HC * E:
                    act.wait_ge(ab_filled, m + 1)
                    if m >= 2:
                        act.wait_ge(h_done, m - 1)
                    act.activation(gate[:, m % 2, :], s_bank[m % 2][:, 0:CAP], ACT.Silu).then_inc(gate_done, 1)
                if 1 <= m <= HC * E:
                    k = m - 1
                    act.wait_ge(h_done, k + 1)
                    if k >= 4:
                        act.wait_ge(w3_done, k - 3)
                    act.activation(h_hi[:, k % 4, :], h32[:, k % 2, :], ACT.Copy).then_inc(h_hi_done, 1)
                if m % HC == 3 and m // HC + 1 < E:
                    expert_in(m // HC + 1)
                if m % HC == 2 and m >= HC:
                    expert_out(m // HC - 1)
            for b in range(B):
                act.wait_ge(fin_done, TR * (b + 1))
                act.dma_start(out_d[b], zo[:, b % 2]).then_inc(stored[b % 2], 16)

        @block.vector
        def _(ve):
            steps = [0]

            def link(ins):
                steps[0] += 1
                ins.then_inc(chain, 1)
                ve.wait_ge(chain, steps[0])

            ve.wait_ge(wp_split_hi, 1)
            ve.tensor_tensor(wp_lo[:].rearrange("p a b -> p (a b)"), p32[:, 0, :],
                             wp_hi[:].rearrange("p a b -> p (a b)"), ALU.subtract).then_inc(wp_split, 1)
            ve.wait_ge(consts_in, 16 * 12)
            ve.wait_ge(zeroed, 17)

            def low_p(n):
                ve.wait_ge(p_hi_done, n + 1)
                if n >= 2:
                    ve.wait_ge(o_filled, n - 1)
                ve.tensor_tensor(p_lo[:, n % 2, :], p32[:, n % 2, :], p_hi[:, n % 2, :],
                                 ALU.subtract).then_inc(p_lo_done, 1)

            def normalise(n):
                ve.wait_ge(o_filled, n + 1)
                o = o_bank[n % 2][:, 0:NG * OC].rearrange("p (g c) -> p g c", g=NG)
                link(ve.reciprocal(rden[:], o[:, :, 64:66]))
                link(ve.tensor_tensor(rmask[:], rden[:].unsqueeze(3).to_broadcast([P, NG, 2, HG]),
                                      small[:, 0:4].unsqueeze(1).unsqueeze(1).to_broadcast([P, NG, 2, HG]), ALU.mult))
                if n >= 2:
                    ve.wait_ge(o_lo_done, n - 1)
                ve.tensor_tensor(o32[:, n % 2, :].rearrange("p (g a c) -> p g a c", g=NG, a=8),
                                 o[:, :, 0:64].rearrange("p g (a c) -> p g a c", a=8),
                                 rmask[:].rearrange("p g s h -> p g (s h)").unsqueeze(3).to_broadcast([P, NG, 8, HD]),
                                 ALU.mult).then_inc(o32_done, 1)

            def route(b):
                ve.wait_ge(spare_filled, count("LG", b))
                ve.tensor_tensor(lg[:], mb(("LG", b))[:, 0:TR * E].rearrange("p (t e) -> p t e", e=E),
                                 bg_row[:].unsqueeze(1).to_broadcast([P, TR, E]), ALU.add).then_inc(spare_free, 1)
                ve.wait_ge(spare_free, count("LG", b))
                rev = small[:, 8:16].unsqueeze(1).to_broadcast([P, TR, E])
                for k in range(2):
                    link(ve.tensor_reduce(top[:, k, :], lg[:], AX, ALU.max))
                    link(ve.tensor_tensor(tmp[:], lg[:], top[:, k, :].unsqueeze(2).to_broadcast([P, TR, E]), ALU.is_equal))
                    link(ve.tensor_tensor(tmp[:], tmp[:], rev, ALU.mult))
                    link(ve.tensor_reduce(pos[:, k, :], tmp[:], AX, ALU.max))
                    link(ve.tensor_tensor(pick[:, k], pos[:, k, :].unsqueeze(2).to_broadcast([P, TR, E]), rev, ALU.is_equal))
                    if k == 0:
                        link(ve.scalar_tensor_tensor(out=lg[:], in0=pick[:, 0], scalar=-3.0e38, in1=lg[:],
                                                     op0=ALU.mult, op1=ALU.add))
                ve.tensor_tensor(label[:], pick[:, 0], pick[:, 1], ALU.add).then_inc(label_done, 1)
                ve.tensor_tensor(gap[:], top[:, 1, :], top[:, 0, :], ALU.subtract).then_inc(gap_done, 1)

            def place(b):
                ve.wait_ge(spare_filled, count("RK", b))
                m = mb(("RK", b))
                link(ve.tensor_tensor(seq[:], m[:, 0:TR * E].rearrange("p (t e) -> p t e", e=E),
                                      base[:].unsqueeze(1).to_broadcast([P, TR, E]), ALU.add))
                ve.tensor_tensor(base[:], m[:, TR * E:TR * E + E], base[:], ALU.add).then_inc(spare_free, 1)
                for k in range(2):
                    link(ve.tensor_tensor(tmp[:], seq[:], pick[:, k], ALU.mult))
                    link(ve.tensor_reduce(slot[:, k, :], tmp[:], AX, ALU.add))
                link(ve.tensor_scalar(flat[:], pos[:], -float(CAP), float(E * CAP - 1), ALU.mult, ALU.add))
                link(ve.tensor_tensor(flat[:], flat[:], slot[:], ALU.add))
                link(ve.tensor_scalar(valid[:], slot[:], float(CAP), None, ALU.is_le))
                tok = small[:, 16 + b * TR:16 + (b + 1) * TR]
                for k in range(2):
                    link(ve.tensor_scalar(slot[:, k, :], tok, float(E * CAP + k * T), None, ALU.add))
                link(ve.tensor_tensor(flat[:], flat[:], slot[:], ALU.subtract))
                link(ve.tensor_tensor(flat[:], flat[:], valid[:], ALU.mult))
                if b >= 1:
                    ve.wait_ge(sent[(b - 1) % 2], 16 * TR * 2 * ((b - 1) // 2 + 1))
                link(ve.tensor_tensor(index[:], flat[:], slot[:], ALU.add))
                ve.wait_ge(egap_done, b + 1)
                link(ve.tensor_scalar(wgt[:, 0, :], egap[:], 1.0, None, ALU.add))
                xa, xb = x2a[:, b * TR:(b + 1) * TR, D:ROW], x2b[:, :, D:ROW]
                link(ve.reciprocal(xa[:, :, 0], wgt[:, 0, :]))
                link(ve.tensor_tensor(xb[:, :, 0], xa[:, :, 0], egap[:], ALU.mult))
                link(ve.tensor_copy(xa[:, :, 1], tok))
                ve.wait_ge(x2b_done, b + 1)
                ve.tensor_scalar(xb[:, :, 1], tok, float(T), None, ALU.add).then_inc(rows_done, 1)

            for u in range(ROUNDS):
                if u < NU:
                    if u % 2 == 0:
                        b = u // 2
                        ve.wait_ge(xT_hi_done, b + 1)
                        ve.tensor_tensor(xT_lo[:, b % 2, HALF:HALF + S], mb(("xT", b))[:, :],
                                         xT_hi[:, b % 2, HALF:HALF + S], ALU.subtract).then_inc(spare_free, 1)
                        for i, what in enumerate("qk"):
                            ve.wait_ge(qk_hi_done, 2 * b + i + 1)
                            ve.scalar_tensor_tensor(out=qk_lo[:, i, :], in0=mb((what, b))[:, :], scalar=bias[:, i:i + 1],
                                                    in1=qk_hi[:, i, :], op0=ALU.add, op1=ALU.subtract).then_inc(spare_free, 1)
                    v = mb(("V", u))[:, :].rearrange("p (a c) -> p a c", c=32)
                    ve.wait_ge(vx_hi_done, 2 * u + 2)
                    link(ve.tensor_tensor(vx_lo[0:64, u % 2, :, 0:32], v[0:64], vx_hi[0:64, u % 2, :, 0:32], ALU.subtract))
                    ve.tensor_tensor(vx_lo[64:128, u % 2, :, 32:64], v[64:128], vx_hi[64:128, u % 2, :, 32:64],
                                     ALU.subtract).then_inc(spare_free, 1)
                for j in range(4):
                    if u < NU:
                        n = 4 * u + j
                        ve.wait_ge(s_filled, n + 1)
                        ve.tensor_reduce(nmax[:, u % 2, 8 * j:8 * j + 8], s_bank[n % 2][:, :].rearrange("p (a k) -> p a k", k=KW),
                                         AX, ALU.max, negate=True).then_inc(s_maxed, 1)
                    if 1 <= u <= NU:
                        low_p(4 * (u - 1) + j)
                        if j >= 1:
                            normalise(4 * (u - 1) + j - 1)
                    for what, i in after_step(u, j):
                        if what == "AT":
                            ve.wait_ge(at_hi_done, i + 1)
                            ve.scalar_tensor_tensor(out=at_lo[:], in0=mb((what, i))[:, 0:UT], scalar=bias[:, 2:3],
                                                    in1=at_hi[:], op0=ALU.add, op1=ALU.subtract).then_inc(spare_free, 1)
                        if what == "WO":
                            if i == 0:
                                ve.wait_ge(tables_in, 16 * 4)
                            ve.wait_ge(spare_filled, count(what, i))
                            ve.wait_ge(bo_added, i // 2 + 1)
                            ve.tensor_tensor(res[:], mb((what, i))[:, 0:UT].rearrange("p (t d) -> p t d", t=2),
                                             x_sb[:, 2 * i:2 * i + 2, :], ALU.add).then_inc(spare_free, 1)
                            ve.wait_ge(spare_free, count(what, i))
                            for t in range(2):
                                link(ve.bn_stats(stats[:, t, :], res[:, t, :]))
                            for t in range(2):
                                link(ve.bn_aggr(mv[:, t, :], stats[:, t, :]))
                            ve.tensor_scalar(vareps[:, 0:2], mv[:, 0:2, 1], EPS, None, ALU.add).then_inc(var_done, 1)
                        if what == "XT2":
                            ve.wait_ge(spare_filled, count(what, i))
                            ve.tensor_copy(x2T[:], mb((what, i))[:, :]).then_inc(spare_free, 1)
                        if what == "LG":
                            route(i)
                        if what == "RK":
                            place(i)
                        if what == "norm":
                            ve.wait_ge(rstd_done, i + 1)
                            for t in range(2):
                                ve.tensor_scalar(x2a[:, 2 * i + t, 0:D], res[:, t, :], mv[:, t, 0:1], rstd[:, t:t + 1],
                                                 ALU.subtract, ALU.mult).then_inc(x2_done, 1)
                            ve.wait_ge(x2_done, 2 * i + 2)
                if u < NU:
                    ve.wait_ge(s_maxed, 4 * u + 4)
                    ve.tensor_copy(nmax2[:, 0, :], nmax[:, u % 2, :]).then_inc(nmax_hi, 1)
                    ve.wait_ge(nmax_hi, u + 1)
                    ve.tensor_tensor(nmax2[:, 1, :], nmax[:, u % 2, :], nmax2[:, 0, :], ALU.subtract).then_inc(nmax_split, 1)
                if 1 <= u <= NU:
                    normalise(4 * (u - 1) + 3)
                if u < NU:
                    ve.wait_ge(spare_filled, count("mT", u))
                    ve.tensor_copy(mT[0:64, u % 2, :], mb(("mT", u))[0:64, 0:64].bitcast(BF16)).then_inc(spare_free, 1)

            def expert_in(e):
                ve.wait_ge(xeT_hi_done, e + 1)
                ve.tensor_tensor(xeT_lo[:, e % 2, :], m_bank[0][:, 0:CAP], xeT_hi[:, e % 2, :].bitcast(F32),
                                 ALU.subtract).then_inc(xeT_split, 1)
                if e >= 3:
                    ve.wait_ge(returned[(e - 3) % 2], 48 * ((e - 3) // 2 + 1))
                ve.wait_ge(xe_in[e % 3], 32 * (e // 3 + 1))
                ve.tensor_copy(ret[:, e % 3, 0:2], xe[:, e % 3, 0:2, D + 1]).then_inc(ret_done, 1)
                ve.tensor_copy(ret[0:64, e % 3, 2:3], xe[0:64, e % 3, 2, D + 1:D + 2]).then_inc(ret_done, 1)

            def expert_back(e):
                ve.wait_ge(yb_filled, e + 1)
                if e >= 2:
                    ve.wait_ge(returned[e % 2], 48 * (e // 2))
                for j in range(3):
                    n = P if j < 2 else 64
                    ve.tensor_scalar(ye[0:n, e % 2, j, :], m_bank[1][0:n, j * D:(j + 1) * D], xe[0:n, e % 3, j, D:D + 1],
                                     None, ALU.mult).then_inc(ye_done, 1)

            expert_in(0)
            for m in range(HC * E + 5):
                if m < HC * E:
                    ve.wait_ge(gate_done, m + 1)
                    if m >= 2:
                        ve.wait_ge(h_hi_done, m - 1)
                        ve.wait_ge(h_split, m - 1)
                    ve.tensor_tensor(h32[:, m % 2, :], gate[:, m % 2, :], t_bank[m % 2][:, 0:CAP], ALU.mult).then_inc(h_done, 1)
                if 1 <= m <= HC * E:
                    k = m - 1
                    ve.wait_ge(h_hi_done, k + 1)
                    if k >= 4:
                        ve.wait_ge(w3_done, k - 3)
                    ve.tensor_tensor(h_lo[:, k % 4, :], h32[:, k % 2, :], h_hi[:, k % 4, :].bitcast(F32),
                                     ALU.subtract).then_inc(h_split, 1)
                if m % HC == 3 and m // HC + 1 < E:
                    expert_in(m // HC + 1)
                if m % HC == 0 and m >= 2 * HC:
                    expert_back(m // HC - 2)
            for b in range(B):
                ve.wait_ge(y_in[b % 2], 32 * (b // 2 + 1))
                link(ve.tensor_tensor(z[:, b % 2], y01[:, b % 2, 0], y01[:, b % 2, 1], ALU.add))
                link(ve.tensor_tensor(z[:, b % 2], z[:, b % 2], x2a[:, b * TR:(b + 1) * TR, 0:D], ALU.add))
                for t in range(TR):
                    link(ve.bn_stats(stats[:, t, :], z[:, b % 2, t, :]))
                for t in range(TR):
                    link(ve.bn_aggr(mv[:, t, :], stats[:, t, :]))
                ve.tensor_scalar(vareps[:], mv[:, :, 1], EPS, None, ALU.add).then_inc(fin_var, 1)
                ve.wait_ge(fin_rstd, b + 1)
                if b >= 2:
                    ve.wait_ge(stored[b % 2], 16 * (b // 2))
                for t in range(TR):
                    ve.tensor_scalar(zo[:, b % 2, t, :], z[:, b % 2, t, :], mv[:, t, 0:1], rstd[:, t:t + 1],
                                     ALU.subtract, ALU.mult).then_inc(fin_done, 1)

        @block.tensor
        def _(pe):
            def spare_bank(use):
                if spare[use] >= 2:
                    pe.wait_ge(spare_free, spare[use] - 1)
                return mb(use)

            def scores_q(n):
                u, j = divmod(n, 4)
                if n >= 2:
                    pe.wait_ge(s_maxed, n - 1)
                if j == 0:
                    pe.wait_ge(qx_done, HG * (u + 1))
                    pe.wait_ge(k3_in, 16 * 12 * (u // 2 + 1))
                bank, b, blk = s_bank[n % 2], u // 2, (u % 2) * UB + 2 * j
                pe.matmul(bank[:, :].rearrange("p (s g k) -> p s g k", s=2, g=NG), onehot[:],
                          mask[:, blk:blk + 2, :].unsqueeze(2).to_broadcast([QB, 2, NG, KW]),
                          start=True, stop=False, skip_group_check=True)
                for s in range(2):
                    for g in range(NG):
                        c = (s * NG + g) * KW
                        mm = pe.matmul(bank[:, c:c + KW], qx[:, u % 2, g, 2 * j + s, :],
                                       k3[:, b % 2, g, QB * (blk + s):QB * (blk + s) + KW],
                                       start=False, stop=True, skip_group_check=True)
                mm.then_inc(s_filled, 1)

            def scores_k(n):
                u, j = divmod(n, 4)
                b, half = divmod(u, 2)
                if j == 0:
                    pe.wait_ge(spare_free, count("mT", u))
                if n >= 2:
                    pe.wait_ge(p_hi_done, n - 1)
                bank = t_bank[n % 2]
                for g in range(NG):
                    pe.matmul(bank[:, g * P:(g + 1) * P], aux[:, half, j, g, :], mT[:, u % 2, :],
                              start=(g == 0), stop=False, skip_group_check=True)
                for s, blk in enumerate(PAIRS[j]):
                    key = QB * (half * UB + blk)
                    for g in range(NG):
                        mm = pe.matmul(bank[KW * s:KW * s + KW, g * P:(g + 1) * P],
                                       k3[:, b % 2, g, key:key + KW], qx[:, u % 2, g, blk, :],
                                       start=False, stop=True, skip_group_check=True)
                mm.then_inc(t_filled, 1)

            def output(n):
                u, j = divmod(n, 4)
                pe.wait_ge(p_lo_done, n + 1)
                if j == 0:
                    pe.wait_ge(spare_free, count("V", u))
                if n >= 2:
                    pe.wait_ge(o32_done, n - 1)
                for g in range(NG):
                    o = o_bank[n % 2][:, g * OC:(g + 1) * OC]
                    hi, lo = p_hi[:, n % 2, g * P:(g + 1) * P], p_lo[:, n % 2, g * P:(g + 1) * P]
                    pe.matmul(o, hi, vx_hi[:, u % 2, j * NG + g, :], start=True, stop=False)
                    pe.matmul(o, hi, vx_lo[:, u % 2, j * NG + g, :], start=False, stop=False)
                    mm = pe.matmul(o, lo, vx_hi[:, u % 2, j * NG + g, :], start=False, stop=True)
                mm.then_inc(o_filled, 1)

            pe.wait_ge(consts_in, 16 * 12)
            pe.wait_ge(zeroed, 17)
            for u in range(ROUNDS):
                if u < NU:
                    b = u // 2
                    if u % 2 == 0:
                        m = spare_bank(("xT", b))
                        pe.wait_ge(x_in[b], 16)
                        for t in range(TR):
                            mm = pe.transpose(m[:, t * P:(t + 1) * P], x_sb[:, b * TR + t, :], ident[:])
                        mm.then_inc(spare_filled, 1)
                        for i, what in enumerate("qk"):
                            m = spare_bank((what, b))
                            if i == 0:
                                pe.wait_ge(spare_free, count("xT", b))
                                pe.wait_ge(wp_split, 1)
                            xh, xl = (t[:, b % 2, HALF:HALF + S] for t in (xT_hi, xT_lo))
                            pe.matmul(m[:, :], wp_hi[:, i, :], xh, start=True, stop=False)
                            pe.matmul(m[:, :], wp_hi[:, i, :], xl, start=False, stop=False)
                            pe.matmul(m[:, :], wp_lo[:, i, :], xh, start=False, stop=True).then_inc(spare_filled, 1)
                    m = spare_bank(("V", u))
                    for i, (first, _) in enumerate(PAIRS):
                        key = QB * ((u % 2) * UB + first)
                        xh, xl = (t[:, b % 2, key:key + P] for t in (xT_hi, xT_lo))
                        o = m[:, i * D:(i + 1) * D]
                        pe.matmul(o, xh, wp_hi[:, 2, :], start=True, stop=False)
                        pe.matmul(o, xh, wp_lo[:, 2, :], start=False, stop=False)
                        mm = pe.matmul(o, xl, wp_hi[:, 2, :], start=False, stop=True)
                    mm.then_inc(spare_filled, 1)
                for j in range(4):
                    if u < NU:
                        scores_q(4 * u + j)
                    if 1 <= u <= NU:
                        if u == 1 and j == 0:
                            pe.wait_ge(tables_in, 16 * 4)
                            pe.wait_ge(mT_rows_in, 32)
                        scores_k(4 * (u - 1) + j)
                        if j >= 1:
                            output(4 * (u - 1) + j - 1)
                    for what, i in after_step(u, j):
                        if what not in PSUM_USES:
                            continue
                        m = spare_bank((what, i))
                        if what == "AT":
                            pe.wait_ge(o_lo_done, 4 * i + 4)
                            for k, pair in enumerate(PAIRS):
                                for s, blk in enumerate(pair):
                                    o = m[:, blk * QB:(blk + 1) * QB]
                                    pe.matmul(o, o_hi[:, k, s, :], merge[:], start=True, stop=False)
                                    mm = pe.matmul(o, o_lo[:, k, s, :], merge[:], start=False, stop=True)
                        if what == "WO":
                            pe.wait_ge(spare_free, count("AT", i))
                            for t in range(2):
                                o, ah, al = m[:, t * D:(t + 1) * D], at_hi[:, t * P:(t + 1) * P], at_lo[:, t * P:(t + 1) * P]
                                pe.matmul(o, ah, wp_hi[:, 3, :], start=True, stop=False)
                                pe.matmul(o, ah, wp_lo[:, 3, :], start=False, stop=False)
                                mm = pe.matmul(o, al, wp_hi[:, 3, :], start=False, stop=True)
                        if what == "XT2":
                            pe.wait_ge(x2_done, 4 * i + 4)
                            for t in range(TR):
                                mm = pe.transpose(m[:, t * P:(t + 1) * P], x2a[:, i * TR + t, 0:D], ident[:])
                        if what == "LG":
                            pe.wait_ge(spare_free, count("XT2", i))
                            for t in range(TR):
                                mm = pe.matmul(m[:, t * E:(t + 1) * E], x2T[:, t * P:(t + 1) * P], wg[:], start=True, stop=True)
                        if what == "RK":
                            pe.wait_ge(label_done, i + 1)
                            for t in range(TR):
                                o = m[:, t * E:(t + 1) * E]
                                for s in range(t + 1):
                                    pe.matmul(o, tri[:] if s == t else ones[:], label[:, s, :], start=(s == 0), stop=(s == t))
                            for t in range(TR):
                                mm = pe.matmul(m[:, TR * E:(TR + 1) * E], ones[:], label[:, t, :], start=(t == 0), stop=(t == TR - 1))
                        mm.then_inc(spare_filled, 1)
                if 1 <= u <= NU:
                    output(4 * (u - 1) + 3)
                if u < NU:
                    m = spare_bank(("mT", u))
                    pe.wait_ge(nmax_split, u + 1)
                    pe.transpose(m[0:64, 0:64].bitcast(BF16), nmax2[:].rearrange("p s c -> p (s c)"),
                                 identb[:]).then_inc(spare_filled, 1)

            def expert_in(e):
                pe.wait_ge(xe_in[e % 3], 32 * (e // 3 + 1))
                if e == 0:
                    pe.wait_ge(spare_free, len(spare))
                if e >= 1:
                    pe.wait_ge(xeT_split, e)
                for j in range(3):
                    n = P if j < 2 else 64
                    mm = pe.transpose(m_bank[0][:, j * P:j * P + n], xe[0:n, e % 3, j, 0:D], ident[0:n, 0:n])
                mm.then_inc(xeT_filled, 1)

            def up(m):
                e, c = divmod(m, HC)
                if c == 0:
                    pe.wait_ge(xeT_split, e + 1)
                if m == 0:
                    pe.wait_ge(w_split, 3 * E)
                if m >= 2:
                    pe.wait_ge(h_done, m - 1)
                xh, xl = xeT_hi[:, e % 2, :], xeT_lo[:, e % 2, :]
                for bank, first in ((s_bank[m % 2], 0), (t_bank[m % 2], H)):
                    cols = slice(first + c * P, first + (c + 1) * P)
                    pe.matmul(bank[:, 0:CAP], w_hi[:, e, cols], xh, start=True, stop=False)
                    pe.matmul(bank[:, 0:CAP], w_hi[:, e, cols], xl, start=False, stop=False)
                    mm = pe.matmul(bank[:, 0:CAP], w_lo[:, e, cols], xh, start=False, stop=True)
                mm.then_inc(ab_filled, 1)

            def down(m):
                e, c = divmod(m, HC)
                pe.wait_ge(h_split, m + 1)
                if c == 0 and e >= 2:
                    pe.wait_ge(yT_done, e - 1)
                cols = slice(2 * H + c * P, 2 * H + (c + 1) * P)
                o = o_bank[e % 2][:, 0:CAP]
                pe.matmul(o, w_hi[:, e, cols], h_hi[:, m % 4, :], start=(c == 0), stop=False)
                pe.matmul(o, w_hi[:, e, cols], h_lo[:, m % 4, :], start=False, stop=False)
                mm = pe.matmul(o, w_lo[:, e, cols], h_hi[:, m % 4, :], start=False, stop=(c == HC - 1))
                mm.then_inc(w3_done, 1)

            def expert_back(e):
                pe.wait_ge(yT_done, e + 1)
                if e >= 1:
                    pe.wait_ge(ye_done, 3 * e)
                for j in range(3):
                    n = P if j < 2 else 64
                    mm = pe.transpose(m_bank[1][0:n, j * D:(j + 1) * D], yT[:, e % 2, j * P:j * P + n], ident[:])
                mm.then_inc(yb_filled, 1)

            expert_in(0)
            for m in range(HC * E + 4):
                if m < HC * E:
                    up(m)
                if 2 <= m < HC * E + 2:
                    down(m - 2)
                if m % HC == 2 and m // HC + 1 < E:
                    expert_in(m // HC + 1)
                if m % HC == 3 and m >= HC + 3 :
                    expert_back(m // HC - 1)


PSUM_USES = ("AT", "WO", "XT2", "LG", "RK")


def after_step(u, j):
    uses = []
    unit = u - 2
    if 0 <= unit < NU:
        if j == 0:
            uses.append(("AT", unit))
        if j == 1:
            uses.append(("WO", unit))
        if j == 2:
            uses.append(("norm", unit))
        if j == 3 and unit % 2:
            uses += [("copy", unit // 2), ("XT2", unit // 2)]
    unit = u - 3
    if 0 <= unit < NU and unit % 2:
        if j == 0:
            uses.append(("LG", unit // 2))
        if j == 1:
            uses.append(("RK", unit // 2))
    return uses


_INS = ["L0_attn_x", "L0_attn_Wq", "L0_attn_bq", "L0_attn_Wk", "L0_attn_bk", "L0_attn_Wv", "L0_attn_bv",
        "L0_attn_Wo", "L0_attn_bo", "L0_ffn_Wg", "L0_ffn_bg", "L0_ffn_W1", "L0_ffn_W2", "L0_ffn_W3"]


def kernel(**inputs):
    import concourse.bacc as bacc
    from concourse.bass_utils import run_bass_kernel_spmd

    nc = bacc.Bacc("TRN2", target_bir_lowering=False, num_devices=1)
    arrays = {name: np.ascontiguousarray(inputs[name]) for name in _INS}
    arrays.update(constants())
    args = [nc.dram_tensor(name, a.shape, mybir.dt.from_np(a.dtype), kind="ExternalInput").ap()
            for name, a in arrays.items()]
    out = nc.dram_tensor("out", [B, S, D], F32, kind="ExternalOutput").ap()
    layer_kernel(nc, *args, out)
    results = run_bass_kernel_spmd(nc, [arrays], core_ids=[0])
    return results.results[0]["out"]
```

```python
from contextlib import ExitStack

import numpy as np

import concourse.bass as bass
from concourse import mybir

ALU = mybir.AluOpType
ACT = mybir.ActivationFunctionType
AX = mybir.AxisListType.X
F32 = mybir.dt.float32
F32R = mybir.dt.float32r
FP16 = mybir.dt.float16
BF16 = mybir.dt.bfloat16
I32 = mybir.dt.int32

P = 128
B, S, D = 4, 512, 128
T = B * S
NT = T // P
NH, HD = 16, 8
HG, NG = 4, 4
HALF = 16
QB, KW = 32, 64
UB = 8
UT = UB * QB
NU = T // UT
PAIRS = [(0, 2), (1, 3), (4, 6), (5, 7)]
SP = S + 2 * HALF
NTERM = 3
KR = NTERM * HG * HD
OC = 2 * HG * HD + 2
E, H, CAP = 8, 512, 320
HC = H // P
ROW = D + 2
TR = S // P
GROUPS = [(0, 4), (4, 4), (8, 4), (12, 2), (14, 2)]
ROUNDS = NU + 3
SM_HEAD, SM_ROW, SM_REV, SM_TOK, SM_DUMP, SM_FLAT, SM = 0, 4, 8, 16, 32, 64, 96
LAG = 3
BIG = -1.0e30
SCALE = float(HD) ** -0.5
EPS = 1e-5


def constants():
    def bf16(a):
        return (np.ascontiguousarray(a, dtype=np.float32).view(np.uint32) >> 16).astype(np.uint16)

    p = np.arange(P)
    c = {}
    j, k = np.arange(QB)[:, None, None], np.arange(KW)[None, None, :]
    b = np.arange(S // QB)[None, :, None]
    key = QB * b - HALF + k
    seen = (k >= j) & (k <= j + 2 * HALF) & (key >= 0) & (key < S)
    mask = np.where(seen, 0.0, BIG)
    onehot = p[None, :] % QB == np.arange(QB)[:, None]
    half = np.zeros((P, 4 * P + QB + (S // QB) * KW), np.uint16)
    half[:, 0:P] = bf16(np.eye(P))
    half[:, P:2 * P] = bf16(p[:, None] <= p[None, :])
    half[0:QB, 2 * P:3 * P] = half[64:96, 2 * P:3 * P] = bf16(onehot)
    half[:, 3 * P:3 * P + QB] = onehot.T.astype(np.float16).view(np.uint16)
    half[0:QB, 3 * P + QB:3 * P + QB + (S // QB) * KW] = bf16(mask.reshape(QB, -1))
    c["c_half"] = half
    aux = np.zeros((96, 2, 4, NG, P), np.float32)
    for half in range(2):
        for i, pair in enumerate(PAIRS):
            for g in range(NG):
                for s, blk in enumerate(pair):
                    cols = slice(KW * s, KW * s + KW)
                    aux[blk * NG + g, half, i, g, cols] = 1
                    aux[32 + blk * NG + g, half, i, g, cols] = 1
                    aux[64:96, half, i, g, cols] = mask[:, half * UB + blk, :]
    c["c_aux"] = bf16(aux.reshape(96, -1))
    f = np.zeros((P, P + SM), np.float32)
    f[:, 0:P] = np.eye(P)
    f[:, P + SM_HEAD:P + SM_HEAD + HG] = p[:, None] // QB == np.arange(HG)
    f[:, P + SM_ROW:P + SM_ROW + HG] = (p[:, None] % 32) // HD == np.arange(HG)
    f[:, P + SM_REV:P + SM_REV + E] = E - np.arange(E)
    token = p[:, None] + P * np.arange(NT)
    f[:, P + SM_TOK:P + SM_TOK + NT] = token
    for k in range(2):
        f[:, P + SM_DUMP + k * NT:P + SM_DUMP + (k + 1) * NT] = E * CAP + k * T + token
        f[:, P + SM_FLAT + k * NT:P + SM_FLAT + (k + 1) * NT] = E * CAP + k * T + token + 1
    c["c_f32"] = f
    d = np.zeros((E * CAP, ROW), np.float32)
    d[:, D + 1] = 2 * T + np.arange(E * CAP)
    c["c_disp"] = d
    return c


def layer_kernel(nc, x, w_proj, b_rows, W1, W2, W3, c_half, c_aux, c_f32, c_disp, out):
    x_d = x.rearrange("b (t p) d -> b p t d", p=P)
    out_d = out.rearrange("b (t p) d -> b p t d", p=P)
    disp = nc.dram_tensor("dispatched", [E * CAP + 2 * T, ROW], F32).ap()
    back = nc.dram_tensor("returned", [2 * T + E * CAP, D], F32).ap()

    parts = nc.dram_tensor("qk_parts", [B, 2, 2, P, S], FP16).ap()

    order = [("xT", 0), ("q", 0), ("k", 0)]
    for u in range(ROUNDS):
        for j in range(4):
            order += [use for use in after_step(u, j) if use[0] in PSUM_USES]
        if u < NU:
            order += [("mT", u)]
    spare = {use: n for n, use in enumerate(order)}

    with ExitStack() as ctx:
        def sem(name):
            return ctx.enter_context(nc.semaphore(name))

        def sb(name, shape, dt, c=ctx):
            return c.enter_context(nc.sbuf_tensor(name, shape, dt))

        def ps(name, dt=F32):
            return ctx.enter_context(nc.psum_tensor(name, [P, 512], dt))

        w_hi = sb("w_hi", [P, E, 3 * H], F32R)
        w_lo = sb("w_lo", [P, E, 3 * H], F32R)
        w_raw = sb("w_raw", [P, 3, H], F32)
        x2a = sb("x2a", [P, NT, ROW], F32)
        x2b = sb("x2b", [P, TR, ROW], F32)
        f32c = sb("f32c", [P, P + SM], F32)
        ident, small = f32c[:, 0:P], f32c[:, P:P + SM]
        stats = sb("stats", [P, 4, 6], F32)
        mv = sb("mv", [P, 4, 2], F32)
        vareps = sb("vareps", [P, 4], F32)
        rstd = sb("rstd", [P, 4], F32)
        mhalf = sb("mhalf", [P, 4], F32)
        shift = sb("shift", [P, 4], F32)

        actx = ExitStack()
        x_sb = sb("x_sb", [P, NT, D], F32, actx)
        xT_hi = sb("xT_hi", [P, 2, SP], FP16, actx)
        xT_lo = sb("xT_lo", [P, 2, SP], FP16, actx)
        wp_hi = sb("wp_hi", [P, 4, D], FP16, actx)
        wp_lo = sb("wp_lo", [P, 4, D], FP16, actx)
        qk_hi = sb("qk_hi", [P, 2, S], FP16, actx)
        qk_lo = sb("qk_lo", [P, 2, S], FP16, actx)
        w_proj_sb = sb("w_proj_sb", [P, 4 * D + E + 3], F32, actx)
        wg, bias = w_proj_sb[:, 4 * D:4 * D + E], w_proj_sb[:, 4 * D + E:4 * D + E + 3]
        q3 = sb("q3", [KR, NG, S], FP16, actx)
        k3 = sb("k3", [KR, 2, NG, SP], FP16, actx)
        qx = sb("qx", [KR, 2, NG, UB, HG * QB], FP16, actx)
        vx_hi = sb("vx_hi", [P, 2, 4 * NG, OC], FP16, actx)
        vx_lo = sb("vx_lo", [P, 2, 4 * NG, OC], FP16, actx)
        p32 = sb("p32", [P, 2, 512], F32, actx)
        p_hi = sb("p_hi", [P, 2, 512], FP16, actx)
        p_lo = sb("p_lo", [P, 2, 512], FP16, actx)
        o32 = sb("o32", [P, 2, NG * 64], F32, actx)
        o_hi = sb("o_hi", [P, 4, 2, P], FP16, actx)
        o_lo = sb("o_lo", [P, 4, 2, P], FP16, actx)
        rden = sb("rden", [P, NG, 2], F32, actx)
        rmask = sb("rmask", [P, NG, 2, HG], F32, actx)
        nmax = sb("nmax", [P, 2, UB * NG], F32, actx)
        nmax2 = sb("nmax2", [P, 2, UB * NG], BF16, actx)
        mT = sb("mT", [96, 2, P], BF16, actx)
        at_hi = sb("at_hi", [P, UT], FP16, actx)
        at_lo = sb("at_lo", [P, UT], FP16, actx)
        res = sb("res", [P, 2, D], F32, actx)
        x2T = sb("x2T", [P, S], F32, actx)
        half = sb("half", [P, 4 * P + QB + (S // QB) * KW], BF16, actx)
        identb, tri, onehot = half[:, 0:P], half[:, P:2 * P], half[0:QB, 2 * P:3 * P]
        merge = half[:, 3 * P:3 * P + QB].bitcast(FP16)
        mask = half[0:QB, 3 * P + QB:3 * P + QB + (S // QB) * KW].rearrange("j (b k) -> j b k", k=KW)
        aux = sb("aux", [96, 2, 4, NG, P], BF16, actx)
        ones = sb("ones", [P, P], BF16, actx)
        rows = sb("rows", [P, D + E], F32, actx)
        lg = sb("lg", [P, TR, E], F32, actx)
        tmp = sb("tmp", [P, TR, E], F32, actx)
        pick = sb("pick", [P, 2, TR, E], F32, actx)
        top = sb("top", [P, 2, TR], F32, actx)
        pos = sb("pos", [P, 2, TR], F32, actx)
        label = sb("label", [P, TR, E], BF16, actx)
        seq = sb("seq", [P, TR, E], F32, actx)
        base = sb("base", [P, E], F32, actx)
        slot = sb("slot", [P, 2, TR], F32, actx)
        flat = sb("flat", [P, 2, TR], F32, actx)
        valid = sb("valid", [P, 2, TR], F32, actx)
        gap = sb("gap", [P, TR], F32, actx)
        egap = sb("egap", [P, TR], F32, actx)
        wgt = sb("wgt", [P, 2, TR], F32, actx)
        index = sb("index", [P, 2, TR], I32, actx)
        zero = sb("zero", [P, D], F32, actx)
        actx.close()

        ectx = ExitStack()
        xe = sb("xe", [P, 4, 3, ROW], F32, ectx)
        xeT_hi = sb("xeT_hi", [P, 2, CAP], F32R, ectx)
        xeT_lo = sb("xeT_lo", [P, 2, CAP], F32R, ectx)
        gate = sb("gate", [P, 2, CAP], F32, ectx)
        h32 = sb("h32", [P, 2, CAP], F32, ectx)
        h_hi = sb("h_hi", [P, 4, CAP], F32R, ectx)
        h_lo = sb("h_lo", [P, 4, CAP], F32R, ectx)
        yT = sb("yT", [P, 2, CAP], F32, ectx)
        ye = sb("ye", [P, 2, 3, D], F32, ectx)
        ret = sb("ret", [P, 4, 3], I32, ectx)
        y01 = sb("y01", [P, B, 2, TR, D], F32, ectx)
        z = sb("z", [P, B, TR, D], F32, ectx)
        zo = sb("zo", [P, B, TR, D], F32, ectx)
        ectx.close()

        s_bank = [ps("s_bank0"), ps("s_bank1")]
        t_bank = [ps("t_bank0"), ps("t_bank1")]
        o_bank = [ps("o_bank0"), ps("o_bank1")]
        m_bank = [ps("m_bank0"), ps("m_bank1")]

        def mb(use):
            return m_bank[spare[use] % 2]

        def count(*use):
            return spare[use] + 1

        x_in = [sem(f"x_in{b}") for b in range(B)]
        wp_in, consts_in, aux_in, rows_in = map(sem, ("wp_in", "consts_in", "aux_in", "rows_in"))
        mT_rows, ret_rows = sem("mT_rows"), sem("ret_rows")
        zeroed, dram_set = sem("zeroed"), sem("dram_set")
        wp_split_hi, wp_split = sem("wp_split_hi"), sem("wp_split")
        spare_filled, spare_free = sem("spare_filled"), sem("spare_free")
        xT_hi_done = sem("xT_hi_done")
        qk_hi_done = sem("qk_hi_done")
        q3_in, k3_in = sem("q3_in"), sem("k3_in")
        parts_out = [sem("q_parts_out"), sem("k_parts_out")]
        qx_ve, qx_act, qx_gp = sem("qx_ve"), sem("qx_act"), sem("qx_gp")
        vx_hi_done = sem("vx_hi_done")
        s_filled, s_maxed = sem("s_filled"), sem("s_maxed")
        nmax_hi, nmax_split = sem("nmax_hi"), sem("nmax_split")
        t_filled, p32_done, p_hi_done, p_lo_done = map(sem, ("t_filled", "p32_done", "p_hi_done", "p_lo_done"))
        o_filled, o32_done, o_hi_done, o_lo_done = map(sem, ("o_filled", "o32_done", "o_hi_done", "o_lo_done"))
        at_hi_done = sem("at_hi_done")
        bo_added = sem("bo_added")
        var_done, rstd_done, x2_done, x2b_done = map(sem, ("var_done", "rstd_done", "x2_done", "x2b_done"))
        gap_done, egap_done, label_done = map(sem, ("gap_done", "egap_done", "label_done"))
        slot_done, index_done, rows_done, x2a_rows = map(sem, ("slot_done", "index_done", "rows_done", "x2a_rows"))
        sent = [sem(f"sent{i}") for i in range(len(GROUPS))]
        w_in = [sem(f"w_in{i}") for i in range(3)]
        w_hi_done, w_split = sem("w_hi_done"), sem("w_split")
        xe_in = [sem(f"xe_in{i}") for i in range(4)]
        xeT_filled, xeT_hi_done, xeT_split = map(sem, ("xeT_filled", "xeT_hi_done", "xeT_split"))
        ab_filled, gate_done, h_done, h_hi_done, h_split = map(sem, ("ab_filled", "gate_done", "h_done", "h_hi_done", "h_split"))
        w3_done, yT_done, yb_filled, ye_done, ret_done = map(sem, ("w3_done", "yT_done", "yb_filled", "ye_done", "ret_done"))
        returned = [sem("returned_even"), sem("returned_odd")]
        y_in = [sem(f"y_in{b}") for b in range(B)]
        y_sum, fin_var, fin_rstd, fin_done = sem("y_sum"), sem("fin_var"), sem("fin_rstd"), sem("fin_done")
        stored = sem("stored")
        chain, gp_chain = sem("vector_chain"), sem("gpsimd_chain")

        block = ctx.enter_context(nc.Block())

        def expand_wait(engine, u, half):
            engine.wait_ge(q3_in, 16 * NTERM * (u // 2 + 1))
            if u >= 2:
                engine.wait_ge(t_filled, 4 * (u - 2) + 2 * half + 2)

        def expand_aps(u, half, h):
            first = (u % 2) * UB + 4 * half
            src = q3[:, :, first * QB:(first + 4) * QB].rearrange("p g (b q) -> p g b q", q=QB)
            return src, qx[:, u % 2, :, 4 * half:4 * half + 4, h * QB:(h + 1) * QB]

        def expanded(u, half):
            n = 2 * u + half + 1
            return (qx_ve, 2 * n), (qx_act, n), (qx_gp, n)

        @block.sync
        def _(sp):
            for b in range(B):
                sp.dma_start(x_sb[:, b * TR:(b + 1) * TR, :], x_d[b]).then_inc(x_in[b], 16)
                if b == 0:
                    sp.dma_start(f32c[:], c_f32).then_inc(consts_in, 16)
                    sp.dma_start(w_proj_sb[:], w_proj).then_inc(wp_in, 16)
                    sp.dma_start(half[:], c_half.bitcast(BF16)).then_inc(consts_in, 16)

            def parts_write(b, i):
                sp.wait_ge(spare_free, count("qk"[i], b))
                for part, t in enumerate((qk_hi, qk_lo)):
                    sp.dma_start(parts[b, part, i], t[:, i, :]).then_inc(parts_out[i], 16)

            def parts_read(b, i):
                sp.wait_ge(parts_out[i], 32 * (b + 1))
                if i == 0 and b >= 1:
                    sp.wait_ge(qx_ve, 2 * 2 * 2 * b)
                    sp.wait_ge(qx_act, 2 * 2 * b)
                    sp.wait_ge(qx_gp, 2 * 2 * b)
                if i == 1 and b >= 2:
                    sp.wait_ge(s_filled, 8 * (b - 1))
                    sp.wait_ge(t_filled, 8 * (b - 1))
                for term in range(NTERM):
                    to = (q3[32 * term:32 * term + 32, :, :] if i == 0 else
                          k3[32 * term:32 * term + 32, b % 2, :, HALF:HALF + S])
                    src = parts[b, 1 if term == 1 + i else 0, i].rearrange("(g r) t -> r g t", g=NG)
                    sp.dma_start(to, src).then_inc((q3_in, k3_in)[i], 16)

            def w_load(n):
                e, part = divmod(n, 3)
                if n >= 3:
                    sp.wait_ge(w_split, n - 2)
                dst, src = w_raw[:, n % 3, :], (W1, W2, W3)[part][e]
                if part == 2:
                    dst, src = dst.rearrange("p (c d) -> p c d", c=HC), src.rearrange("(c p) d -> p c d", p=P)
                sp.dma_start(dst, src).then_inc(w_in[part], 16)

            parts_write(0, 0)
            parts_write(0, 1)
            parts_read(0, 0)
            parts_read(0, 1)
            sp.dma_start(aux[:].rearrange("p a b c d -> p (a b c d)"), c_aux.bitcast(BF16)).then_inc(aux_in, 16)
            sp.dma_start(rows[:], b_rows.partition_broadcast(P)).then_inc(rows_in, 16)
            sp.dma_start(disp[0:E * CAP, :], c_disp).then_inc(dram_set, 16)
            sp.wait_ge(zeroed, 1)
            sp.dma_start(back[0:2 * T, :].rearrange("(p r) d -> p r d", p=P),
                         zero[:].unsqueeze(1).to_broadcast([P, 2 * T // P, D])).then_inc(dram_set, 16)
            for u in range(NU):
                for i in range(3):
                    w_load(3 * u + i)
                b = u // 2 + 1
                if u % 2 == 0 and b < B:
                    parts_write(b, 0)
                    parts_write(b, 1)
                    parts_read(b, 1)
                    parts_read(b, 0)

            for e in range(E):
                if e == 0:
                    for i, (_, n) in enumerate(GROUPS):
                        sp.wait_ge(sent[i], 16 * 2 * n)
                if e >= 4:
                    sp.wait_ge(ye_done, 3 * (e - 3))
                    sp.wait_ge(ret_done, 2 * (e - 3))
                filled = disp[e * CAP:(e + 1) * CAP, :]
                sp.dma_start(xe[:, e % 4, 0:2, :], filled[0:256, :].rearrange("(j p) d -> p j d", p=P)).then_inc(xe_in[e % 4], 16)
                sp.dma_start(xe[0:64, e % 4, 2, :], filled[256:CAP, :]).then_inc(xe_in[e % 4], 16)
            for i in range(2):
                sp.wait_ge(returned[i], 48 * E // 2)
            for b in range(B):
                for i in range(2):
                    src = back[i * T + b * S:i * T + (b + 1) * S, :].rearrange("(t p) d -> p t d", p=P)
                    sp.dma_start(y01[:, b, i], src).then_inc(y_in[b], 16)
            sp.wait_ge(stored, 16 * B)

        @block.gpsimd
        def _(gp):
            gp.memset(zero[:], 0.0).then_inc(zeroed, 1)
            gp.memset(mhalf[:], -0.5).then_inc(zeroed, 1)
            gp.memset(ones[:], 1.0).then_inc(zeroed, 1)
            gp.memset(base[:], 0.0).then_inc(zeroed, 1)
            for t in (xT_hi, xT_lo):
                for i in range(2):
                    gp.memset(t[:, i, 0:HALF], 0.0).then_inc(zeroed, 1)
                    gp.memset(t[:, i, HALF + S:SP], 0.0).then_inc(zeroed, 1)
            for i in range(2):
                gp.memset(k3[:, i, :, 0:HALF], 0.0).then_inc(zeroed, 1)
                gp.memset(k3[:, i, :, HALF + S:SP], 0.0).then_inc(zeroed, 1)
            gp.memset(vx_lo[:], 0.0).then_inc(zeroed, 1)
            gp.memset(vx_hi[:], 0.0).then_inc(gp_chain, 1)
            gp.wait_ge(gp_chain, 1)
            gp.memset(vx_hi[0:64, :, :, 64:65], 1.0).then_inc(zeroed, 1)
            gp.memset(vx_hi[64:128, :, :, 65:66], 1.0).then_inc(zeroed, 1)
            gp.wait_ge(consts_in, 32)
            for i in range(2):
                gp.tensor_scalar(mT[64:96, i, :], half[64:96, 2 * P:3 * P], 1.0, 0.0, ALU.mult, ALU.add).then_inc(mT_rows, 1)
            gp.wait_ge(mT_rows, 2)
            gp.tensor_scalar(x2a[:, :, D + 1], small[:, SM_TOK:SM_TOK + NT], 1.0, 0.0, ALU.mult, ALU.add).then_inc(x2a_rows, 1)

            def w_split_third(n):
                e, part = divmod(n, 3)
                gp.wait_ge(w_in[part], 16 * (e + 1))
                cols = slice(part * H, (part + 1) * H)
                gp.wait_ge(w_hi_done, n + 1)
                gp.tensor_tensor(w_lo[:, e, cols], w_raw[:, n % 3, :], w_hi[:, e, cols].bitcast(F32),
                                 ALU.subtract).then_inc(w_split, 1)

            def o_low(n):
                j = n % 4
                gp.wait_ge(o_hi_done, n + 1)
                gp.tensor_tensor(o_lo[:, j].rearrange("p s (g c) -> p s g c", g=NG),
                                 o32[:, n % 2, :].rearrange("p (g s c) -> p s g c", g=NG, s=2),
                                 o_hi[:, j].rearrange("p s (g c) -> p s g c", g=NG),
                                 ALU.subtract).then_inc(o_lo_done, 1)

            steps = [1]

            def link(ins):
                steps[0] += 1
                ins.then_inc(gp_chain, 1)
                gp.wait_ge(gp_chain, steps[0])

            def expand(u, half):
                if u < NU:
                    expand_wait(gp, u, half)
                    src, dst = expand_aps(u, half, 3)
                    gp.tensor_scalar(dst, src, small[0:KR, SM_ROW + 3:SM_ROW + 4], 1.0, ALU.mult, ALU.mult).then_inc(qx_gp, 1)

            def send(i):
                first, n = GROUPS[i]
                off = first % TR
                f, v, sl, ix = flat[:, :, 0:n], valid[:, :, 0:n], slot[:, :, 0:n], index[:, :, off:off + n]
                table = lambda at: small[:, at:at + 2 * NT].rearrange("p (k t) -> p k t", k=2)[:, :, first:first + n]
                gp.wait_ge(slot_done, i + 1)
                link(gp.tensor_scalar(f, pos[:, :, 0:n], -float(CAP), float(E * CAP), ALU.mult, ALU.add))
                link(gp.tensor_tensor(f, f, sl, ALU.add))
                link(gp.tensor_tensor(f, f, table(SM_FLAT), ALU.subtract))
                link(gp.tensor_scalar(v, sl, float(CAP), 1.0, ALU.is_le, ALU.mult))
                link(gp.tensor_tensor(f, f, v, ALU.mult))
                link(gp.tensor_tensor(f, f, table(SM_DUMP), ALU.add))
                if i >= 1 and off == 0:
                    gp.wait_ge(sent[i - 1], 16 * 2 * GROUPS[i - 1][1])
                link(gp.tensor_copy(ix, f))
                gp.tensor_scalar(x2b[:, off:off + n, D + 1], small[:, SM_TOK + first:SM_TOK + first + n], float(T), 1.0,
                                 ALU.add, ALU.mult).then_inc(index_done, 1)
                gp.wait_ge(index_done, i + 1)
                gp.wait_ge(rows_done, i + 1)
                gp.wait_ge(x2b_done, i + 1)
                if i == 0:
                    gp.wait_ge(dram_set, 32)
                for t in range(n):
                    for k in range(2):
                        gp.indirect_dma_start(
                            disp, bass.IndirectOffsetOnAxis(ap=index[:, k, off + t:off + t + 1], axis=0),
                            x2a[:, first + t, :] if k == 0 else x2b[:, off + t, :], None).then_inc(sent[i], 16)

            def add_bias(b):
                gp.wait_ge(spare_filled, count("xT", b))
                xb = x_sb[:, b * TR:(b + 1) * TR, :]
                gp.tensor_tensor(xb, xb, rows[:, 0:D].unsqueeze(1).to_broadcast([P, TR, D]), ALU.add).then_inc(bo_added, 1)

            expand(0, 0)
            expand(0, 1)
            gp.wait_ge(rows_in, 16)
            add_bias(0)
            for u in range(ROUNDS):
                for j in range(4):
                    if 1 <= u <= NU and j < 3:
                        w_split_third(3 * (u - 1) + j)
                    if 1 <= u <= NU and j >= 1:
                        o_low(4 * (u - 1) + j - 1)
                    if j == 2 and u + 1 < NU:
                        expand(u + 1, 0)
                    for what, i in after_step(u, j):
                        if what == "WO":
                            gp.wait_ge(var_done, i + 1)
                            gp.tensor_tensor(rstd[:, 0:2], vareps[:, 0:2], mhalf[:, 0:2], ALU.pow).then_inc(rstd_done, 1)
                        if what == "q":
                            add_bias(i)
                        if what == "RK":
                            send(i)
                if 1 <= u <= NU:
                    o_low(4 * (u - 1) + 3)
                if u + 1 < NU:
                    expand(u + 1, 1)

            for e in range(E):
                gp.wait_ge(ye_done, 3 * (e + 1))
                gp.wait_ge(ret_done, 2 * (e + 1))
                for j in range(3):
                    n = P if j < 2 else 64
                    gp.indirect_dma_start(
                        back, bass.IndirectOffsetOnAxis(ap=ret[0:n, e % 4, j:j + 1], axis=0),
                        ye[0:n, e % 2, j, :], None).then_inc(returned[e % 2], 16)
            for b in range(B + 1):
                if b < B:
                    gp.wait_ge(y_in[b], 32)
                    gp.tensor_tensor(y01[:, b, 0], y01[:, b, 0], y01[:, b, 1], ALU.add).then_inc(y_sum, 1)
                if b >= 1:
                    gp.wait_ge(fin_var, b)
                    if b >= 2:
                        gp.wait_ge(fin_done, TR * (b - 1))
                    link(gp.tensor_tensor(rstd[:], vareps[:], mhalf[:], ALU.pow))
                    link(gp.tensor_tensor(shift[:], mv[:, :, 0], rstd[:], ALU.mult))
                    gp.tensor_scalar(shift[:], shift[:], -1.0, 0.0, ALU.mult, ALU.add).then_inc(fin_rstd, 1)

        @block.scalar
        def _(act):
            def o_high(n):
                act.wait_ge(o32_done, n + 1)
                if n % 4 == 0 and n >= 4:
                    act.wait_ge(spare_filled, count("AT", n // 4 - 1))
                act.activation(o_hi[:, n % 4].rearrange("p s (g c) -> p s g c", g=NG),
                               o32[:, n % 2, :].rearrange("p (g s c) -> p s g c", g=NG, s=2), ACT.Copy).then_inc(o_hi_done, 1)

            def prepare(what, i):
                if what == "xT":
                    act.wait_ge(spare_filled, count(what, i))
                    act.activation(xT_hi[:, i % 2, HALF:HALF + S], mb((what, i))[:, :], ACT.Copy).then_inc(xT_hi_done, 1)
                if what in "qk":
                    c = "qk".index(what)
                    act.wait_ge(spare_filled, count(what, i))
                    if i >= 1:
                        act.wait_ge(parts_out[c], 32 * i)
                    act.activation(qk_hi[:, c, :], mb((what, i))[:, :], ACT.Identity,
                                   bias=bias[:, c:c + 1]).then_inc(qk_hi_done, 1)
                if what == "V":
                    act.wait_ge(spare_filled, count(what, i))
                    v = mb((what, i))[:, :].rearrange("p (a c) -> p a c", c=32)
                    act.activation(vx_hi[0:64, i % 2, :, 0:32], v[0:64], ACT.Copy).then_inc(vx_hi_done, 1)
                    act.activation(vx_hi[64:128, i % 2, :, 32:64], v[64:128], ACT.Copy).then_inc(vx_hi_done, 1)

            def expand(u, half):
                expand_wait(act, u, half)
                src, dst = expand_aps(u, half, 2)
                act.activation(dst, src, ACT.Copy, scale=small[0:KR, SM_ROW + 2:SM_ROW + 3]).then_inc(qx_act, 1)

            act.wait_ge(wp_in, 16)
            act.activation(wp_hi[:].rearrange("p a b -> p (a b)"), w_proj_sb[:, 0:4 * D], ACT.Copy).then_inc(wp_split_hi, 1)
            act.wait_ge(consts_in, 32)
            act.wait_ge(zeroed, 19)
            for what in ("xT", "q", "k"):
                prepare(what, 0)
            expand(0, 0)
            expand(0, 1)
            for u in range(ROUNDS):
                for j in range(4):
                    if 1 <= u <= NU:
                        n = 4 * (u - 1) + j
                        act.wait_ge(t_filled, n + 1)
                        if n >= 2:
                            act.wait_ge(p_lo_done, n - 1)
                            act.wait_ge(o_filled, n - 1)
                        act.activation(p32[:, n % 2, :], t_bank[n % 2][:, :], ACT.Exp, scale=SCALE).then_inc(p32_done, 1)
                        act.activation(p_hi[:, n % 2, :], t_bank[n % 2][:, :], ACT.Exp, scale=SCALE).then_inc(p_hi_done, 1)
                        if j >= 1:
                            o_high(n - 1)
                        if j < 3:
                            w = 3 * (u - 1) + j
                            act.wait_ge(w_in[w % 3], 16 * (w // 3 + 1))
                            act.activation(w_hi[:, w // 3, (w % 3) * H:(w % 3 + 1) * H], w_raw[:, w % 3, :],
                                           ACT.Copy).then_inc(w_hi_done, 1)
                    if j == 2 and u + 1 < NU:
                        expand(u + 1, 0)
                    for what, i in after_step(u, j):
                        if what in ("xT", "q", "k", "V"):
                            prepare(what, i)
                        if what == "AT":
                            act.wait_ge(spare_filled, count(what, i))
                            act.activation(at_hi[:], mb((what, i))[:, 0:UT], ACT.Identity, bias=bias[:, 2:3]).then_inc(at_hi_done, 1)
                        if what == "copy":
                            first, n = GROUPS[i]
                            off = first % TR
                            act.wait_ge(x2_done, first + n)
                            if i >= 1 and off == 0:
                                act.wait_ge(sent[i - 1], 16 * 2 * GROUPS[i - 1][1])
                            act.activation(x2b[:, off:off + n, 0:D], x2a[:, first:first + n, 0:D], ACT.Copy).then_inc(x2b_done, 1)
                        if what == "LG":
                            act.wait_ge(gap_done, i + 1)
                            n = GROUPS[i][1]
                            act.activation(egap[:, 0:n], gap[:, 0:n], ACT.Exp).then_inc(egap_done, 1)
                if 1 <= u <= NU:
                    o_high(4 * (u - 1) + 3)
                if u + 1 < NU:
                    expand(u + 1, 1)

            def expert_in(e):
                act.wait_ge(xeT_filled, e + 1)
                act.activation(xeT_hi[:, e % 2, :], m_bank[0][:, 0:CAP], ACT.Copy).then_inc(xeT_hi_done, 1)

            def expert_out(e):
                act.wait_ge(w3_done, HC * (e + 1))
                if e >= 2:
                    act.wait_ge(yb_filled, e - 1)
                act.activation(yT[:, e % 2, :], o_bank[e % 2][:, 0:CAP], ACT.Copy).then_inc(yT_done, 1)

            expert_in(0)
            for m in range(HC * E + LAG + 1):
                if m < HC * E:
                    act.wait_ge(ab_filled, m + 1)
                    if m >= 2:
                        act.wait_ge(h_done, m - 1)
                    act.activation(gate[:, m % 2, :], s_bank[m % 2][:, 0:CAP], ACT.Silu).then_inc(gate_done, 1)
                if 1 <= m <= HC * E:
                    k = m - 1
                    act.wait_ge(h_done, k + 1)
                    if k >= 4:
                        act.wait_ge(w3_done, k - 3)
                    act.activation(h_hi[:, k % 4, :], h32[:, k % 2, :], ACT.Copy).then_inc(h_hi_done, 1)
                if m % HC == 1 and m // HC + 1 < E:
                    expert_in(m // HC + 1)
                if m % HC == (HC - 1 + LAG) % HC and m >= HC - 1 + LAG:
                    expert_out((m - (HC - 1 + LAG)) // HC)
            for b in range(B):
                act.wait_ge(fin_rstd, b + 1)
                for t in range(TR):
                    act.activation(zo[:, b, t, :], z[:, b, t, :], ACT.Identity, bias=shift[:, t:t + 1],
                                   scale=rstd[:, t:t + 1]).then_inc(fin_done, 1)
                act.wait_ge(fin_done, TR * (b + 1))
                act.dma_start(out_d[b], zo[:, b]).then_inc(stored, 16)

        @block.vector
        def _(ve):
            steps = [0]

            def link(ins):
                steps[0] += 1
                ins.then_inc(chain, 1)
                ve.wait_ge(chain, steps[0])

            ve.wait_ge(wp_split_hi, 1)
            ve.tensor_tensor(wp_lo[:].rearrange("p a b -> p (a b)"), w_proj_sb[:, 0:4 * D],
                             wp_hi[:].rearrange("p a b -> p (a b)"), ALU.subtract).then_inc(wp_split, 1)
            ve.wait_ge(consts_in, 32)
            ve.wait_ge(zeroed, 19)

            def prepare(what, i):
                if what == "xT":
                    ve.wait_ge(xT_hi_done, i + 1)
                    ve.tensor_tensor(xT_lo[:, i % 2, HALF:HALF + S], mb((what, i))[:, :],
                                     xT_hi[:, i % 2, HALF:HALF + S], ALU.subtract).then_inc(spare_free, 1)
                if what in "qk":
                    c = "qk".index(what)
                    ve.wait_ge(qk_hi_done, 2 * i + c + 1)
                    ve.scalar_tensor_tensor(out=qk_lo[:, c, :], in0=mb((what, i))[:, :], scalar=bias[:, c:c + 1],
                                            in1=qk_hi[:, c, :], op0=ALU.add, op1=ALU.subtract).then_inc(spare_free, 1)
                if what == "V":
                    v = mb((what, i))[:, :].rearrange("p (a c) -> p a c", c=32)
                    ve.wait_ge(vx_hi_done, 2 * i + 2)
                    link(ve.tensor_tensor(vx_lo[0:64, i % 2, :, 0:32], v[0:64], vx_hi[0:64, i % 2, :, 0:32], ALU.subtract))
                    ve.tensor_tensor(vx_lo[64:128, i % 2, :, 32:64], v[64:128], vx_hi[64:128, i % 2, :, 32:64],
                                     ALU.subtract).then_inc(spare_free, 1)

            def expand(u, half):
                expand_wait(ve, u, half)
                for h in range(2):
                    src, dst = expand_aps(u, half, h)
                    ve.tensor_scalar(dst, src, small[0:KR, SM_ROW + h:SM_ROW + h + 1], None, ALU.mult).then_inc(qx_ve, 1)

            def low_p(n):
                ve.wait_ge(p_hi_done, n + 1)
                if n >= 2:
                    ve.wait_ge(o_filled, n - 1)
                ve.tensor_tensor(p_lo[:, n % 2, :], p32[:, n % 2, :], p_hi[:, n % 2, :],
                                 ALU.subtract).then_inc(p_lo_done, 1)

            def normalise_first(n):
                ve.wait_ge(o_filled, n + 1)
                o = o_bank[n % 2][:, 0:NG * OC].rearrange("p (g c) -> p g c", g=NG)
                steps[0] += 1
                ve.reciprocal(rden[:], o[:, :, 64:66]).then_inc(chain, 1)

            def normalise(n):
                ve.wait_ge(chain, steps[0])
                o = o_bank[n % 2][:, 0:NG * OC].rearrange("p (g c) -> p g c", g=NG)
                link(ve.tensor_tensor(rmask[:], rden[:].unsqueeze(3).to_broadcast([P, NG, 2, HG]),
                                      small[:, SM_HEAD:SM_HEAD + HG].unsqueeze(1).unsqueeze(1).to_broadcast([P, NG, 2, HG]),
                                      ALU.mult))
                if n >= 2:
                    ve.wait_ge(o_lo_done, n - 1)
                ve.tensor_tensor(o32[:, n % 2, :].rearrange("p (g a c) -> p g a c", g=NG, a=8),
                                 o[:, :, 0:64].rearrange("p g (a c) -> p g a c", a=8),
                                 rmask[:].rearrange("p g s h -> p g (s h)").unsqueeze(3).to_broadcast([P, NG, 8, HD]),
                                 ALU.mult).then_inc(o32_done, 1)

            def route(i):
                n = GROUPS[i][1]
                g, w = lg[:, 0:n], tmp[:, 0:n]
                ve.wait_ge(spare_filled, count("LG", i))
                if i == 0:
                    ve.wait_ge(rows_in, 16)
                if i >= 1:
                    ve.wait_ge(index_done, i)
                ve.tensor_tensor(g, mb(("LG", i))[:, 0:n * E].rearrange("p (t e) -> p t e", e=E),
                                 rows[:, D:D + E].unsqueeze(1).to_broadcast([P, n, E]), ALU.add).then_inc(spare_free, 1)
                ve.wait_ge(spare_free, count("LG", i))
                rev = small[:, SM_REV:SM_REV + E].unsqueeze(1).to_broadcast([P, n, E])
                for k in range(2):
                    link(ve.tensor_reduce(top[:, k, 0:n], g, AX, ALU.max))
                    link(ve.tensor_tensor(w, g, top[:, k, 0:n].unsqueeze(2).to_broadcast([P, n, E]), ALU.is_equal))
                    link(ve.tensor_tensor(w, w, rev, ALU.mult))
                    link(ve.tensor_reduce(pos[:, k, 0:n], w, AX, ALU.max))
                    link(ve.tensor_tensor(pick[:, k, 0:n], pos[:, k, 0:n].unsqueeze(2).to_broadcast([P, n, E]), rev, ALU.is_equal))
                    if k == 0:
                        link(ve.scalar_tensor_tensor(out=g, in0=pick[:, 0, 0:n], scalar=-3.0e38, in1=g,
                                                     op0=ALU.mult, op1=ALU.add))
                ve.tensor_tensor(label[:, 0:n], pick[:, 0, 0:n], pick[:, 1, 0:n], ALU.add).then_inc(label_done, 1)
                ve.tensor_tensor(gap[:, 0:n], top[:, 1, 0:n], top[:, 0, 0:n], ALU.subtract).then_inc(gap_done, 1)

            def place(i):
                first, n = GROUPS[i]
                off = first % TR
                w = tmp[:, 0:n]
                ve.wait_ge(spare_filled, count("RK", i))
                m = mb(("RK", i))
                link(ve.tensor_tensor(seq[:, 0:n], m[:, 0:n * E].rearrange("p (t e) -> p t e", e=E),
                                      base[:].unsqueeze(1).to_broadcast([P, n, E]), ALU.add))
                ve.tensor_tensor(base[:], m[:, TR * E:TR * E + E], base[:], ALU.add).then_inc(spare_free, 1)
                for k in range(2):
                    link(ve.tensor_tensor(w, seq[:, 0:n], pick[:, k, 0:n], ALU.mult))
                    ins = ve.tensor_reduce(slot[:, k, 0:n], w, AX, ALU.add)
                    if k == 0:
                        link(ins)
                    else:
                        ins.then_inc(slot_done, 1)
                ve.wait_ge(egap_done, i + 1)
                if i == 0:
                    ve.wait_ge(x2a_rows, 1)
                ve.wait_ge(x2b_done, i + 1)
                link(ve.tensor_scalar(wgt[:, 0, 0:n], egap[:, 0:n], 1.0, None, ALU.add))
                xa, xb = x2a[:, first:first + n, D], x2b[:, off:off + n, D]
                link(ve.reciprocal(xa, wgt[:, 0, 0:n]))
                ve.tensor_tensor(xb, xa, egap[:, 0:n], ALU.mult).then_inc(rows_done, 1)

            for what in ("xT", "q", "k"):
                prepare(what, 0)
            expand(0, 0)
            expand(0, 1)
            for u in range(ROUNDS):
                for j in range(4):
                    if u < NU:
                        n = 4 * u + j
                        ve.wait_ge(s_filled, n + 1)
                        ve.tensor_reduce(nmax[:, u % 2, 8 * j:8 * j + 8], s_bank[n % 2][:, :].rearrange("p (a k) -> p a k", k=KW),
                                         AX, ALU.max, negate=True).then_inc(s_maxed, 1)
                    if 1 <= u <= NU:
                        if j >= 1:
                            normalise_first(4 * (u - 1) + j - 1)
                        low_p(4 * (u - 1) + j)
                        if j >= 1:
                            normalise(4 * (u - 1) + j - 1)
                    if j == 2 and u + 1 < NU:
                        expand(u + 1, 0)
                    for what, i in after_step(u, j):
                        if what in ("xT", "q", "k", "V"):
                            prepare(what, i)
                        if what == "AT":
                            ve.wait_ge(at_hi_done, i + 1)
                            ve.scalar_tensor_tensor(out=at_lo[:], in0=mb((what, i))[:, 0:UT], scalar=bias[:, 2:3],
                                                    in1=at_hi[:], op0=ALU.add, op1=ALU.subtract).then_inc(spare_free, 1)
                        if what == "WO":
                            ve.wait_ge(spare_filled, count(what, i))
                            ve.wait_ge(bo_added, i // 2 + 1)
                            ve.tensor_tensor(res[:], mb((what, i))[:, 0:UT].rearrange("p (t d) -> p t d", t=2),
                                             x_sb[:, 2 * i:2 * i + 2, :], ALU.add).then_inc(spare_free, 1)
                            ve.wait_ge(spare_free, count(what, i))
                            for t in range(2):
                                link(ve.bn_stats(stats[:, t, :], res[:, t, :]))
                            for t in range(2):
                                link(ve.bn_aggr(mv[:, t, :], stats[:, t, :]))
                            ve.tensor_scalar(vareps[:, 0:2], mv[:, 0:2, 1], EPS, None, ALU.add).then_inc(var_done, 1)
                        if what == "XT2":
                            ve.wait_ge(spare_filled, count(what, i))
                            cols = GROUPS[i][1] * P
                            ve.tensor_copy(x2T[:, 0:cols], mb((what, i))[:, 0:cols]).then_inc(spare_free, 1)
                        if what == "LG":
                            route(i)
                        if what == "RK":
                            place(i)
                        if what == "norm":
                            ve.wait_ge(rstd_done, i + 1)
                            for t in range(2):
                                ve.tensor_scalar(x2a[:, 2 * i + t, 0:D], res[:, t, :], mv[:, t, 0:1], rstd[:, t:t + 1],
                                                 ALU.subtract, ALU.mult).then_inc(x2_done, 1)
                            ve.wait_ge(x2_done, 2 * i + 2)
                if u < NU:
                    ve.wait_ge(s_maxed, 4 * u + 4)
                    ve.tensor_copy(nmax2[:, 0, :], nmax[:, u % 2, :]).then_inc(nmax_hi, 1)
                    ve.wait_ge(nmax_hi, u + 1)
                    ve.tensor_tensor(nmax2[:, 1, :], nmax[:, u % 2, :], nmax2[:, 0, :], ALU.subtract).then_inc(nmax_split, 1)
                if 1 <= u <= NU:
                    normalise_first(4 * (u - 1) + 3)
                    normalise(4 * (u - 1) + 3)
                if u + 1 < NU:
                    expand(u + 1, 1)
                if u < NU:
                    ve.wait_ge(spare_filled, count("mT", u))
                    ve.tensor_copy(mT[0:64, u % 2, :], mb(("mT", u))[0:64, 0:64].bitcast(BF16)).then_inc(spare_free, 1)

            def expert_in(e):
                ve.wait_ge(xeT_hi_done, e + 1)
                ve.tensor_tensor(xeT_lo[:, e % 2, :], m_bank[0][:, 0:CAP], xeT_hi[:, e % 2, :].bitcast(F32),
                                 ALU.subtract).then_inc(xeT_split, 1)
                if e >= 4:
                    ve.wait_ge(returned[e % 2], 48 * ((e - 4) // 2 + 1))
                ve.wait_ge(xe_in[e % 4], 32 * (e // 4 + 1))
                ve.tensor_copy(ret[:, e % 4, 0:2], xe[:, e % 4, 0:2, D + 1]).then_inc(ret_done, 1)
                ve.tensor_copy(ret[0:64, e % 4, 2:3], xe[0:64, e % 4, 2, D + 1:D + 2]).then_inc(ret_done, 1)

            def expert_back(e):
                ve.wait_ge(yb_filled, e + 1)
                if e >= 2:
                    ve.wait_ge(returned[e % 2], 48 * (e // 2))
                for j in range(3):
                    n = P if j < 2 else 64
                    ve.tensor_scalar(ye[0:n, e % 2, j, :], m_bank[1][0:n, j * D:(j + 1) * D], xe[0:n, e % 4, j, D:D + 1],
                                     None, ALU.mult).then_inc(ye_done, 1)

            expert_in(0)
            for m in range(HC * E + LAG + 1):
                if m < HC * E:
                    ve.wait_ge(gate_done, m + 1)
                    if m >= 2:
                        ve.wait_ge(h_hi_done, m - 1)
                        ve.wait_ge(h_split, m - 1)
                    ve.tensor_tensor(h32[:, m % 2, :], gate[:, m % 2, :], t_bank[m % 2][:, 0:CAP], ALU.mult).then_inc(h_done, 1)
                if 1 <= m <= HC * E:
                    k = m - 1
                    ve.wait_ge(h_hi_done, k + 1)
                    if k >= 4:
                        ve.wait_ge(w3_done, k - 3)
                    ve.tensor_tensor(h_lo[:, k % 4, :], h32[:, k % 2, :], h_hi[:, k % 4, :].bitcast(F32),
                                     ALU.subtract).then_inc(h_split, 1)
                if m % HC == 1 and m // HC + 1 < E:
                    expert_in(m // HC + 1)
                if m % HC == (HC + LAG) % HC and m >= HC + LAG:
                    expert_back((m - HC - LAG) // HC)
            for b in range(B):
                ve.wait_ge(y_sum, b + 1)
                link(ve.tensor_tensor(z[:, b], y01[:, b, 0], x2a[:, b * TR:(b + 1) * TR, 0:D], ALU.add))
                for t in range(TR):
                    link(ve.bn_stats(stats[:, t, :], z[:, b, t, :]))
                if b >= 1:
                    ve.wait_ge(fin_rstd, b)
                for t in range(TR):
                    link(ve.bn_aggr(mv[:, t, :], stats[:, t, :]))
                ve.tensor_scalar(vareps[:], mv[:, :, 1], EPS, None, ALU.add).then_inc(fin_var, 1)

        @block.tensor
        def _(pe):
            def spare_bank(use):
                if spare[use] >= 2:
                    pe.wait_ge(spare_free, spare[use] - 1)
                return mb(use)

            def scores_q(n):
                u, j = divmod(n, 4)
                if n >= 2:
                    pe.wait_ge(s_maxed, n - 1)
                if j % 2 == 0:
                    for done, at in expanded(u, j // 2):
                        pe.wait_ge(done, at)
                if j == 0:
                    pe.wait_ge(k3_in, 16 * NTERM * (u // 2 + 1))
                bank, b, blk = s_bank[n % 2], u // 2, (u % 2) * UB + 2 * j
                pe.matmul(bank[:, :].rearrange("p (s g k) -> p s g k", s=2, g=NG), onehot,
                          mask[:, blk:blk + 2, :].unsqueeze(2).to_broadcast([QB, 2, NG, KW]),
                          start=True, stop=False, skip_group_check=True)
                for s in range(2):
                    for g in range(NG):
                        c = (s * NG + g) * KW
                        mm = pe.matmul(bank[:, c:c + KW], qx[:, u % 2, g, 2 * j + s, :],
                                       k3[:, b % 2, g, QB * (blk + s):QB * (blk + s) + KW],
                                       start=False, stop=True, skip_group_check=True)
                mm.then_inc(s_filled, 1)

            def scores_k(n):
                u, j = divmod(n, 4)
                b, half = divmod(u, 2)
                if j == 0:
                    pe.wait_ge(spare_free, count("mT", u))
                if n >= 2:
                    pe.wait_ge(p_hi_done, n - 1)
                bank = t_bank[n % 2]
                for g in range(NG):
                    pe.matmul(bank[:, g * P:(g + 1) * P], aux[:, half, j, g, :], mT[:, u % 2, :],
                              start=(g == 0), stop=False, skip_group_check=True)
                for s, blk in enumerate(PAIRS[j]):
                    key = QB * (half * UB + blk)
                    for g in range(NG):
                        mm = pe.matmul(bank[KW * s:KW * s + KW, g * P:(g + 1) * P],
                                       k3[:, b % 2, g, key:key + KW], qx[:, u % 2, g, blk, :],
                                       start=False, stop=True, skip_group_check=True)
                mm.then_inc(t_filled, 1)

            def output(n):
                u, j = divmod(n, 4)
                pe.wait_ge(p_lo_done, n + 1)
                if j == 0:
                    pe.wait_ge(spare_free, count("V", u))
                if n >= 2:
                    pe.wait_ge(o32_done, n - 1)
                for g in range(NG):
                    o = o_bank[n % 2][:, g * OC:(g + 1) * OC]
                    hi, lo = p_hi[:, n % 2, g * P:(g + 1) * P], p_lo[:, n % 2, g * P:(g + 1) * P]
                    pe.matmul(o, hi, vx_hi[:, u % 2, j * NG + g, :], start=True, stop=False)
                    pe.matmul(o, hi, vx_lo[:, u % 2, j * NG + g, :], start=False, stop=False)
                    mm = pe.matmul(o, lo, vx_hi[:, u % 2, j * NG + g, :], start=False, stop=True)
                mm.then_inc(o_filled, 1)

            def prepare(what, i):
                m = spare_bank((what, i))
                if what == "xT":
                    pe.wait_ge(x_in[i], 16)
                    for t in range(TR):
                        mm = pe.transpose(m[:, t * P:(t + 1) * P], x_sb[:, i * TR + t, :], ident)
                if what in "qk":
                    if what == "q":
                        pe.wait_ge(spare_free, count("xT", i))
                        pe.wait_ge(wp_split, 1)
                    c = "qk".index(what)
                    xh, xl = (t[:, i % 2, HALF:HALF + S] for t in (xT_hi, xT_lo))
                    pe.matmul(m[:, :], wp_hi[:, c, :], xh, start=True, stop=False)
                    pe.matmul(m[:, :], wp_hi[:, c, :], xl, start=False, stop=False)
                    mm = pe.matmul(m[:, :], wp_lo[:, c, :], xh, start=False, stop=True)
                if what == "V":
                    for k, (first, _) in enumerate(PAIRS):
                        key = QB * ((i % 2) * UB + first)
                        xh, xl = (t[:, i // 2 % 2, key:key + P] for t in (xT_hi, xT_lo))
                        o = m[:, k * D:(k + 1) * D]
                        pe.matmul(o, xh, wp_hi[:, 2, :], start=True, stop=False)
                        pe.matmul(o, xh, wp_lo[:, 2, :], start=False, stop=False)
                        mm = pe.matmul(o, xl, wp_hi[:, 2, :], start=False, stop=True)
                mm.then_inc(spare_filled, 1)

            pe.wait_ge(consts_in, 32)
            pe.wait_ge(zeroed, 19)
            for what in ("xT", "q", "k"):
                prepare(what, 0)
            for u in range(ROUNDS):
                for j in range(4):
                    if u < NU:
                        scores_q(4 * u + j)
                    if 1 <= u <= NU:
                        if u == 1 and j == 0:
                            pe.wait_ge(aux_in, 16)
                            pe.wait_ge(mT_rows, 2)
                        scores_k(4 * (u - 1) + j)
                        if j >= 1:
                            output(4 * (u - 1) + j - 1)
                    for what, i in after_step(u, j):
                        if what not in PSUM_USES:
                            continue
                        if what in ("xT", "q", "k", "V"):
                            prepare(what, i)
                            continue
                        m = spare_bank((what, i))
                        first, n = GROUPS[i] if what in ("XT2", "LG", "RK") else (0, 0)
                        if what == "AT":
                            pe.wait_ge(o_lo_done, 4 * i + 4)
                            for k, pair in enumerate(PAIRS):
                                for s, blk in enumerate(pair):
                                    o = m[:, blk * QB:(blk + 1) * QB]
                                    pe.matmul(o, o_hi[:, k, s, :], merge, start=True, stop=False)
                                    mm = pe.matmul(o, o_lo[:, k, s, :], merge, start=False, stop=True)
                        if what == "WO":
                            pe.wait_ge(spare_free, count("AT", i))
                            for t in range(2):
                                o, ah, al = m[:, t * D:(t + 1) * D], at_hi[:, t * P:(t + 1) * P], at_lo[:, t * P:(t + 1) * P]
                                pe.matmul(o, ah, wp_hi[:, 3, :], start=True, stop=False)
                                pe.matmul(o, ah, wp_lo[:, 3, :], start=False, stop=False)
                                mm = pe.matmul(o, al, wp_hi[:, 3, :], start=False, stop=True)
                        if what == "XT2":
                            pe.wait_ge(x2_done, first + n)
                            for t in range(n):
                                mm = pe.transpose(m[:, t * P:(t + 1) * P], x2a[:, first + t, 0:D], ident)
                        if what == "LG":
                            pe.wait_ge(spare_free, count("XT2", i))
                            for t in range(n):
                                mm = pe.matmul(m[:, t * E:(t + 1) * E], x2T[:, t * P:(t + 1) * P], wg, start=True, stop=True)
                        if what == "RK":
                            pe.wait_ge(label_done, i + 1)
                            for t in range(n):
                                o = m[:, t * E:(t + 1) * E]
                                for s in range(t + 1):
                                    pe.matmul(o, tri if s == t else ones[:], label[:, s, :], start=(s == 0), stop=(s == t))
                            for t in range(n):
                                mm = pe.matmul(m[:, TR * E:(TR + 1) * E], ones[:], label[:, t, :], start=(t == 0), stop=(t == n - 1))
                        mm.then_inc(spare_filled, 1)
                if 1 <= u <= NU:
                    output(4 * (u - 1) + 3)
                if u < NU:
                    m = spare_bank(("mT", u))
                    pe.wait_ge(nmax_split, u + 1)
                    pe.transpose(m[0:64, 0:64].bitcast(BF16), nmax2[:].rearrange("p s c -> p (s c)"),
                                 identb).then_inc(spare_filled, 1)

            def expert_in(e):
                pe.wait_ge(xe_in[e % 4], 32 * (e // 4 + 1))
                if e == 0:
                    pe.wait_ge(spare_free, len(spare))
                if e >= 1:
                    pe.wait_ge(xeT_split, e)
                for j in range(3):
                    n = P if j < 2 else 64
                    mm = pe.transpose(m_bank[0][:, j * P:j * P + n], xe[0:n, e % 4, j, 0:D], f32c[0:n, 0:n])
                mm.then_inc(xeT_filled, 1)

            def up(m):
                e, c = divmod(m, HC)
                if c == 0:
                    pe.wait_ge(xeT_split, e + 1)
                if m == 0:
                    pe.wait_ge(w_split, 3 * E)
                if m >= 2:
                    pe.wait_ge(h_done, m - 1)
                xh, xl = xeT_hi[:, e % 2, :], xeT_lo[:, e % 2, :]
                for bank, first in ((s_bank[m % 2], 0), (t_bank[m % 2], H)):
                    cols = slice(first + c * P, first + (c + 1) * P)
                    pe.matmul(bank[:, 0:CAP], w_hi[:, e, cols], xh, start=True, stop=False)
                    pe.matmul(bank[:, 0:CAP], w_hi[:, e, cols], xl, start=False, stop=False)
                    mm = pe.matmul(bank[:, 0:CAP], w_lo[:, e, cols], xh, start=False, stop=True)
                mm.then_inc(ab_filled, 1)

            def down(m):
                e, c = divmod(m, HC)
                pe.wait_ge(h_split, m + 1)
                if c == 0 and e >= 2:
                    pe.wait_ge(yT_done, e - 1)
                cols = slice(2 * H + c * P, 2 * H + (c + 1) * P)
                o = o_bank[e % 2][:, 0:CAP]
                pe.matmul(o, w_hi[:, e, cols], h_hi[:, m % 4, :], start=(c == 0), stop=False)
                pe.matmul(o, w_hi[:, e, cols], h_lo[:, m % 4, :], start=False, stop=False)
                mm = pe.matmul(o, w_lo[:, e, cols], h_hi[:, m % 4, :], start=False, stop=(c == HC - 1))
                mm.then_inc(w3_done, 1)

            def expert_back(e):
                pe.wait_ge(yT_done, e + 1)
                if e >= 1:
                    pe.wait_ge(ye_done, 3 * e)
                for j in range(3):
                    n = P if j < 2 else 64
                    mm = pe.transpose(m_bank[1][0:n, j * D:(j + 1) * D], yT[:, e % 2, j * P:j * P + n], ident)
                mm.then_inc(yb_filled, 1)

            expert_in(0)
            for m in range(HC * E + LAG + 1):
                if m < HC * E:
                    up(m)
                if m % HC == 0 and m // HC + 1 < E:
                    expert_in(m // HC + 1)
                if LAG <= m < HC * E + LAG:
                    down(m - LAG)
                if m % HC == (HC + LAG) % HC and m >= HC + LAG:
                    expert_back((m - HC - LAG) // HC)


PSUM_USES = ("xT", "q", "k", "V", "AT", "WO", "XT2", "LG", "RK")


def after_step(u, j):
    uses = []
    if 0 <= u - 2 < NU:
        if j == 1:
            uses.append(("AT", u - 2))
        if j == 2:
            uses.append(("WO", u - 2))
    if u < NU and j == 0:
        uses.append(("V", u))
    if u < NU and u % 2 == 0 and u // 2 + 1 < B and j >= 1:
        uses.append(("", "xT", "q", "k")[j:j + 1] + (u // 2 + 1,))
    for i, (first, n) in enumerate(GROUPS):
        if first + n == 2 * (u - 3) + 2:
            if j == 2:
                uses.append(("LG", i))
            if j == 3:
                uses.append(("RK", i))
    if 0 <= u - 3 < NU and j == 0:
        uses.append(("norm", u - 3))
        uses += [(what, i) for i, (first, n) in enumerate(GROUPS) if first + n == 2 * (u - 3) + 2
                 for what in ("copy", "XT2")]
    return uses


def kernel(L0_attn_x, L0_attn_Wq, L0_attn_bq, L0_attn_Wk, L0_attn_bk, L0_attn_Wv, L0_attn_bv, L0_attn_Wo, L0_attn_bo,
           L0_ffn_Wg, L0_ffn_bg, L0_ffn_W1, L0_ffn_W2, L0_ffn_W3):
    import concourse.bacc as bacc
    from concourse.bass_utils import run_bass_kernel_spmd

    nc = bacc.Bacc("TRN2", target_bir_lowering=False, num_devices=1)
    biases = [np.asarray(v).reshape(D, 1) for v in (L0_attn_bq, L0_attn_bk, L0_attn_bv)]
    weights = [np.asarray(w) for w in (L0_attn_Wq, L0_attn_Wk, L0_attn_Wv, L0_attn_Wo, L0_ffn_Wg)]
    arrays = {
        "x": np.ascontiguousarray(L0_attn_x),
        "w_proj": np.ascontiguousarray(np.concatenate(weights + biases, axis=1)),
        "b_rows": np.concatenate([np.asarray(L0_attn_bo), np.asarray(L0_ffn_bg)]),
        "W1": np.ascontiguousarray(L0_ffn_W1),
        "W2": np.ascontiguousarray(L0_ffn_W2),
        "W3": np.ascontiguousarray(L0_ffn_W3),
    }
    arrays.update(constants())
    args = [nc.dram_tensor(name, a.shape, mybir.dt.from_np(a.dtype), kind="ExternalInput").ap()
            for name, a in arrays.items()]
    out = nc.dram_tensor("out", [B, S, D], F32, kind="ExternalOutput").ap()
    layer_kernel(nc, *args, out)
    results = run_bass_kernel_spmd(nc, [arrays], core_ids=[0])
    return results.results[0]["out"]
```

```python
from contextlib import ExitStack

import numpy as np

import concourse.bass as bass
from concourse import mybir

ALU = mybir.AluOpType
ACT = mybir.ActivationFunctionType
AX = mybir.AxisListType.X
F32 = mybir.dt.float32
F32R = mybir.dt.float32r
FP16 = mybir.dt.float16
BF16 = mybir.dt.bfloat16
I32 = mybir.dt.int32

P = 128
B, S, D = 4, 512, 128
T = B * S
NT = T // P
NH, HD = 16, 8
HG = 4
NG = NH // HG
HALF = 16
QB, KW = 32, 64
UB = 8
UT = UB * QB
NU = T // UT
PAIRS = [(0, 2), (1, 3), (4, 6), (5, 7)]
SP = S + 2 * HALF
NTERM = 3
KR = NTERM * HG * HD
OC = 2 * HG * HD + 2
E, H, CAP = 8, 512, 320
HC = H // P
ROW = D + 2
TR = S // P
GROUPS = [(0, 2), (2, 4), (6, 4), (10, 2), (12, 2), (14, 2)]
SPU = 4
LAG_K, LAG_P, LAG_O, LAG_H = 4, 5, 6, 7
STEPS = SPU * (NU + 3)
SENDS_LAST = [0, 2, 4, 0, 2 * NT]
LOW_P_GP = [n for n in range(SPU * (NU - 1)) if n % SPU != 3]
HEADS = [{"ve": [0], "act": [2], "gp": [1, 3]}, {"ve": [0], "act": [1, 2], "gp": [3]}]
SPLIT_ACT = 8
SPLIT_VE = 12
SM_HEAD, SM_ROW, SM_REV, SM_TOK, SM_DUMP, SM_FLAT, SM = 0, 4, 8, 16, 32, 64, 96
LAG = 3
BIG = -1.0e30
SCALE = float(HD) ** -0.5
EPS = 1e-5


def constants():
    def bf16(a):
        return (np.ascontiguousarray(a, dtype=np.float32).view(np.uint32) >> 16).astype(np.uint16)

    p = np.arange(P)
    c = {}
    j, k = np.arange(QB)[:, None, None], np.arange(KW)[None, None, :]
    b = np.arange(S // QB)[None, :, None]
    key = QB * b - HALF + k
    seen = (k >= j) & (k <= j + 2 * HALF) & (key >= 0) & (key < S)
    mask = np.where(seen, 0.0, BIG)
    onehot = p[None, :] % QB == np.arange(QB)[:, None]
    half = np.zeros((P, 4 * P + QB + (S // QB) * KW), np.uint16)
    half[:, 0:P] = bf16(np.eye(P))
    half[:, P:2 * P] = bf16(p[:, None] <= p[None, :])
    half[0:QB, 2 * P:3 * P] = half[64:96, 2 * P:3 * P] = bf16(onehot)
    half[:, 3 * P:3 * P + QB] = onehot.T.astype(np.float16).view(np.uint16)
    half[0:QB, 3 * P + QB:3 * P + QB + (S // QB) * KW] = bf16(mask.reshape(QB, -1))
    c["c_half"] = half
    aux = np.zeros((96, 2, 4, NG, P), np.float32)
    for half in range(2):
        for i, pair in enumerate(PAIRS):
            for g in range(NG):
                for s, blk in enumerate(pair):
                    cols = slice(KW * s, KW * s + KW)
                    aux[blk * NG + g, half, i, g, cols] = 1
                    aux[32 + blk * NG + g, half, i, g, cols] = 1
                    aux[64:96, half, i, g, cols] = mask[:, half * UB + blk, :]
    c["c_aux"] = bf16(aux.reshape(96, -1))
    f = np.zeros((P, P + SM), np.float32)
    f[:, 0:P] = np.eye(P)
    f[:, P + SM_HEAD:P + SM_HEAD + HG] = p[:, None] // QB == np.arange(HG)
    f[:, P + SM_ROW:P + SM_ROW + HG] = (p[:, None] % 32) // HD == np.arange(HG)
    f[:, P + SM_REV:P + SM_REV + E] = E - np.arange(E)
    token = p[:, None] + P * np.arange(NT)
    f[:, P + SM_TOK:P + SM_TOK + NT] = token
    for k in range(2):
        f[:, P + SM_DUMP + k * NT:P + SM_DUMP + (k + 1) * NT] = E * CAP + k * T + token
        f[:, P + SM_FLAT + k * NT:P + SM_FLAT + (k + 1) * NT] = E * CAP + k * T + token + 1
    c["c_f32"] = f
    d = np.zeros((E * CAP, ROW), np.float32)
    d[:, D + 1] = 2 * T + np.arange(E * CAP)
    c["c_disp"] = d
    return c


def layer_kernel(nc, x, w_proj, b_rows, W1, W2, W3, c_half, c_aux, c_f32, c_disp, out):
    x_d = x.rearrange("b (t p) d -> b p t d", p=P)
    out_d = out.rearrange("b (t p) d -> b p t d", p=P)
    disp = nc.dram_tensor("dispatched", [E * CAP + 2 * T, ROW], F32).ap()
    back = nc.dram_tensor("returned", [2 * T + E * CAP, D], F32).ap()

    parts = nc.dram_tensor("qk_parts", [B, 2, NTERM, P, S], FP16).ap()

    order = [("xT", 0), ("q", 0), ("k", 0)]
    for s in range(STEPS):
        order += [use for use in after_step(s) if use[0] in PSUM_USES]
    spare = {use: n for n, use in enumerate(order)}

    with ExitStack() as ctx:
        def sem(name):
            return ctx.enter_context(nc.semaphore(name))

        def sb(name, shape, dt, c=ctx):
            return c.enter_context(nc.sbuf_tensor(name, shape, dt))

        def ps(name, dt=F32):
            return ctx.enter_context(nc.psum_tensor(name, [P, 512], dt))

        w_hi = sb("w_hi", [P, E, 3 * H], F32R)
        with ExitStack() as rctx:
            w_raw = sb("w_raw", [P, E, 3 * H], F32, rctx)
        w_lo = sb("w_lo", [P, E, 3 * H], F32R)
        x2a = sb("x2a", [P, NT, ROW], F32)
        x2b = sb("x2b", [P, NT, ROW], F32)
        f32c = sb("f32c", [P, P + SM], F32)
        ident, small = f32c[:, 0:P], f32c[:, P:P + SM]
        stats = sb("stats", [P, 4, 6], F32)
        mv = sb("mv", [P, 4, 2], F32)
        vareps = sb("vareps", [P, 4], F32)
        rstd = sb("rstd", [P, 4], F32)
        mhalf = sb("mhalf", [P, 4], F32)

        actx = ExitStack()
        x_sb = sb("x_sb", [P, NT, D], F32, actx)
        xT_hi = sb("xT_hi", [P, 2, SP], FP16, actx)
        xT_lo = sb("xT_lo", [P, 2, SP], FP16, actx)
        wp_hi = sb("wp_hi", [P, 4, D], FP16, actx)
        wp_lo = sb("wp_lo", [P, 4, D], FP16, actx)
        qk_hi = sb("qk_hi", [P, 2, S], FP16, actx)
        qk_lo = sb("qk_lo", [P, 2, S], FP16, actx)
        w_proj_sb = sb("w_proj_sb", [P, 4 * D + E + 3], F32, actx)
        wg, bias = w_proj_sb[:, 4 * D:4 * D + E], w_proj_sb[:, 4 * D + E:4 * D + E + 3]
        q3 = sb("q3", [KR, NG, S], FP16, actx)
        k3 = sb("k3", [KR, 2, NG, SP], FP16, actx)
        qx = sb("qx", [KR, 2, NG, UB, HG * QB], FP16, actx)
        vx_hi = sb("vx_hi", [P, 2, 4 * NG, OC], FP16, actx)
        vx_lo = sb("vx_lo", [P, 2, 4 * NG, OC], FP16, actx)
        p32 = sb("p32", [P, 2, 512], F32, actx)
        p_hi = sb("p_hi", [P, 2, 512], FP16, actx)
        p_lo = sb("p_lo", [P, 2, 512], FP16, actx)
        o32 = sb("o32", [P, 2, NG * 64], F32, actx)
        o_hi = sb("o_hi", [P, 4, 2, P], FP16, actx)
        o_lo = sb("o_lo", [P, 4, 2, P], FP16, actx)
        rden = sb("rden", [P, NG, 2], F32, actx)
        rmask = sb("rmask", [P, NG, 2, HG], F32, actx)
        nmax = sb("nmax", [P, 2, UB * NG], F32, actx)
        nmax2 = sb("nmax2", [P, 2, UB * NG], BF16, actx)
        mT = sb("mT", [96, 2, P], BF16, actx)
        at_hi = sb("at_hi", [P, UT], FP16, actx)
        at_lo = sb("at_lo", [P, UT], FP16, actx)
        res = sb("res", [P, 2, D], F32, actx)
        x2T = sb("x2T", [P, S], F32, actx)
        half = sb("half", [P, 4 * P + QB + (S // QB) * KW], BF16, actx)
        identb, tri, onehot = half[:, 0:P], half[:, P:2 * P], half[0:QB, 2 * P:3 * P]
        merge = half[:, 3 * P:3 * P + QB].bitcast(FP16)
        mask = half[0:QB, 3 * P + QB:3 * P + QB + (S // QB) * KW].rearrange("j (b k) -> j b k", k=KW)
        aux = sb("aux", [96, 2, 4, NG, P], BF16, actx)
        ones = sb("ones", [P, P], BF16, actx)
        rows = sb("rows", [P, D + E], F32, actx)
        lg = sb("lg", [P, TR, E], F32, actx)
        tmp = sb("tmp", [P, 2, TR, E], F32, actx)
        pick = sb("pick", [P, 2, TR, E], F32, actx)
        top = sb("top", [P, TR, E], F32, actx)
        pos = sb("pos", [P, 2, TR], F32, actx)
        label = sb("label", [P, TR, E], BF16, actx)
        seq = sb("seq", [P, TR, E], F32, actx)
        base = sb("base", [P, E], F32, actx)
        slot = sb("slot", [P, 2, TR], F32, actx)
        flat = sb("flat", [P, 2, TR], F32, actx)
        valid = sb("valid", [P, 2, TR], F32, actx)
        gap = sb("gap", [P, TR], F32, actx)
        egap = sb("egap", [P, TR], F32, actx)
        wgt = sb("wgt", [P, 2, TR], F32, actx)
        index = sb("index", [P, 2, NT], I32, actx)
        zero = sb("zero", [P, D], F32, actx)
        actx.close()

        ectx = ExitStack()
        xe = sb("xe", [P, 4, 3, ROW], F32, ectx)
        xeT_hi = sb("xeT_hi", [P, 2, CAP], F32R, ectx)
        xeT_lo = sb("xeT_lo", [P, 2, CAP], F32R, ectx)
        gate = sb("gate", [P, 2, CAP], F32, ectx)
        h32 = sb("h32", [P, 2, CAP], F32, ectx)
        h_hi = sb("h_hi", [P, 4, CAP], F32R, ectx)
        h_lo = sb("h_lo", [P, 4, CAP], F32R, ectx)
        yT = sb("yT", [P, 2, CAP], F32, ectx)
        ye = sb("ye", [P, 2, 3, D], F32, ectx)
        ret = sb("ret", [P, 4, 3], I32, ectx)
        y01 = sb("y01", [P, B, 2, TR, D], F32, ectx)
        z = sb("z", [P, B, TR, D], F32, ectx)
        zo = sb("zo", [P, B, TR, D], F32, ectx)
        fmv = sb("fmv", [P, B, TR, 2], F32, ectx)
        fvar = sb("fvar", [P, B, TR], F32, ectx)
        frstd = sb("frstd", [P, B, TR], F32, ectx)
        fshift = sb("fshift", [P, B, TR], F32, ectx)
        ectx.close()

        s_bank = [ps("s_bank0"), ps("s_bank1")]
        t_bank = [ps("t_bank0"), ps("t_bank1")]
        o_bank = [ps("o_bank0"), ps("o_bank1")]
        m_bank = [ps("m_bank0"), ps("m_bank1")]

        def mb(use):
            return m_bank[spare[use] % 2]

        def count(*use):
            return spare[use] + 1

        x_in = [sem(f"x_in{b}") for b in range(B)]
        wp_in, f32c_in, half_in, aux_in, rows_in = map(sem, ("wp_in", "f32c_in", "half_in", "aux_in", "rows_in"))
        mT_rows = sem("mT_rows")
        zeroed, dram_set = sem("zeroed"), sem("dram_set")
        wp_split_hi, wp_split = sem("wp_split_hi"), sem("wp_split")
        spare_filled, spare_free = sem("spare_filled"), sem("spare_free")
        xT_hi_done = sem("xT_hi_done")
        qk_hi_done = sem("qk_hi_done")
        q3_in, k3_in = sem("q3_in"), sem("k3_in")
        parts_out = [[sem(f"{c}_{part}_out") for part in ("high", "low")] for c in "qk"]
        qx_ve, qx_act, qx_gp = sem("qx_ve"), sem("qx_act"), sem("qx_gp")
        vx_hi_done = sem("vx_hi_done")
        s_filled, s_maxed = sem("s_filled"), sem("s_maxed")
        nmax_hi, nmax_split = sem("nmax_hi"), sem("nmax_split")
        t_filled, p32_done, p_hi_done = map(sem, ("t_filled", "p32_done", "p_hi_done"))
        p_lo_done = [sem("p_lo_even_done"), sem("p_lo_odd_done")]
        o_filled, o32_done, o_hi_done, o_lo_done = map(sem, ("o_filled", "o32_done", "o_hi_done", "o_lo_done"))
        at_hi_done = sem("at_hi_done")
        bo_added = sem("bo_added")
        var_done, rstd_done, x2_done, x2b_done = map(sem, ("var_done", "rstd_done", "x2_done", "x2b_done"))
        gap_done, egap_done, label_done = map(sem, ("gap_done", "egap_done", "label_done"))
        slot_done, index_done, rows_done, return_rows = map(sem, ("slot_done", "index_done", "rows_done", "return_rows"))
        sent = [sem(f"sent{i}") for i in range(len(GROUPS))]
        w_in = [sem(f"w_in{n}") for n in range(3 * E)]
        w_hi_done, w_split_gp, w_split_ve = map(sem, ("w_hi_done", "w_split_gp", "w_split_ve"))
        xe_in = [sem(f"xe_in{i}") for i in range(4)]
        xeT_filled, xeT_hi_done, xeT_split = map(sem, ("xeT_filled", "xeT_hi_done", "xeT_split"))
        ab_filled, gate_done, h_done, h_hi_done, h_split = map(sem, ("ab_filled", "gate_done", "h_done", "h_hi_done", "h_split"))
        w3_done, yT_done, yb_filled, ye_done, ret_done = map(sem, ("w3_done", "yT_done", "yb_filled", "ye_done", "ret_done"))
        returned = [sem("returned_even"), sem("returned_odd")]
        y0_in, y1_in = [sem(f"y0_in{b}") for b in range(B)], [sem(f"y1_in{b}") for b in range(B)]
        y_sum, fin_var, fin_shift, fin_rstd, fin_done = map(sem, ("y_sum", "fin_var", "fin_shift", "fin_rstd", "fin_done"))
        stored, silu_set = sem("stored"), sem("silu_set")
        last_done = sem("last_done")
        chain, gp_chain = sem("vector_chain"), sem("gpsimd_chain")

        block = ctx.enter_context(nc.Block())

        def expand_wait(engine, u, half):
            engine.wait_ge(q3_in, 16 * NTERM * (u // 2 + 1))
            if u >= 2:
                engine.wait_ge(t_filled, 4 * (u - 2) + 2 * half + 2)

        def expand_aps(u, half, h):
            first = (u % 2) * UB + 4 * half
            src = q3[:, :, first * QB:(first + 4) * QB].rearrange("p g (b q) -> p g b q", q=QB)
            return src, qx[:, u % 2, :, 4 * half:4 * half + 4, h * QB:(h + 1) * QB]

        def expanded(u, half):
            count_of = lambda engine: sum(len(heads[engine]) for heads in (HEADS * (u + 1))[:2 * u + half + 1])
            return [(done, count_of(engine)) for engine, done in (("ve", qx_ve), ("act", qx_act), ("gp", qx_gp))]

        def low_p(engine, n):
            engine.wait_ge(p_hi_done, n + 1)
            if n >= 2:
                engine.wait_ge(o_filled, n - 1)
            engine.tensor_tensor(p_lo[:, n % 2, :], p32[:, n % 2, :], p_hi[:, n % 2, :],
                                 ALU.subtract).then_inc(p_lo_done[n % 2], 1)

        @block.sync
        def _(sp):
            def x_load(b):
                sp.dma_start(x_sb[:, b * TR:(b + 1) * TR, :], x_d[b]).then_inc(x_in[b], 16)

            x_load(0)
            sp.dma_start(f32c[:], c_f32).then_inc(f32c_in, 16)
            sp.dma_start(w_proj_sb[:], w_proj).then_inc(wp_in, 16)
            sp.dma_start(half[:], c_half.bitcast(BF16)).then_inc(half_in, 16)
            x_load(1)

            def parts_write(b, i):
                for part, t in enumerate((qk_hi, qk_lo)):
                    if part == 0:
                        sp.wait_ge(qk_hi_done, 2 * b + i + 1)
                        terms, copies = (slice(0, 3, 2), slice(0, 2))[i], 2
                    else:
                        sp.wait_ge(spare_free, count("qk"[i], b))
                        terms, copies = slice(1 + i, 2 + i), 1
                    sp.dma_start(parts[b, i, terms].rearrange("n p t -> p n t"),
                                 t[:, i, :].unsqueeze(1).to_broadcast([P, copies, S])).then_inc(parts_out[i][part], 16)

            def parts_read(b, i):
                for part in range(2):
                    sp.wait_ge(parts_out[i][part], 16 * (b + 1))
                if i == 0 and b >= 1:
                    for done, at in expanded(2 * b - 1, 1):
                        sp.wait_ge(done, at)
                if i == 1 and b >= 2:
                    sp.wait_ge(s_filled, 8 * (b - 1))
                    sp.wait_ge(t_filled, 8 * (b - 1))
                for term in range(NTERM):
                    to = (q3[32 * term:32 * term + 32, :, :] if i == 0 else
                          k3[32 * term:32 * term + 32, b % 2, :, HALF:HALF + S])
                    src = parts[b, i, term].rearrange("(g r) t -> r g t", g=NG)
                    sp.dma_start(to, src).then_inc((q3_in, k3_in)[i], 16)

            def w_load(n):
                e, part = divmod(n, 3)
                dst, src = w_raw[:, e, part * H:(part + 1) * H], (W1, W2, W3)[part][e]
                if part == 2:
                    dst, src = dst.rearrange("p (c d) -> p c d", c=HC), src.rearrange("(c p) d -> p c d", p=P)
                sp.dma_start(dst, src).then_inc(w_in[n], 16)

            parts_write(0, 0)
            parts_write(0, 1)
            parts_read(0, 0)
            parts_read(0, 1)
            sp.dma_start(rows[:], b_rows.partition_broadcast(P)).then_inc(rows_in, 16)
            sp.dma_start(aux[:].rearrange("p a b c d -> p (a b c d)"), c_aux.bitcast(BF16)).then_inc(aux_in, 16)
            w_load(0)
            x_load(2)
            x_load(3)
            for n in range(1, 3 * E):
                w_load(n)
                if n % 7 == 1 and n // 7 + 1 < B:
                    b = n // 7 + 1
                    parts_write(b, 0)
                    parts_write(b, 1)
                    parts_read(b, 1)
                    parts_read(b, 0)
                    if b == 1:
                        sp.dma_start(disp[0:E * CAP, :], c_disp).then_inc(dram_set, 16)
                        sp.wait_ge(zeroed, 1)
                        sp.dma_start(back[0:2 * T, :].rearrange("(p r) d -> p r d", p=P),
                                     zero[:].unsqueeze(1).to_broadcast([P, 2 * T // P, D])).then_inc(dram_set, 16)

            for e in range(E):
                if e == 0:
                    for i, (_, n) in enumerate(GROUPS):
                        sp.wait_ge(sent[i], 16 * 2 * n)
                if e >= 4:
                    sp.wait_ge(ye_done, 3 * (e - 3))
                    sp.wait_ge(ret_done, 2 * (e - 3))
                filled = disp[e * CAP:(e + 1) * CAP, :]
                sp.dma_start(xe[:, e % 4, 0:2, :], filled[0:256, :].rearrange("(j p) d -> p j d", p=P)).then_inc(xe_in[e % 4], 16)
                sp.dma_start(xe[0:64, e % 4, 2, :], filled[256:CAP, :]).then_inc(xe_in[e % 4], 16)
            for i in range(2):
                sp.wait_ge(returned[i], 48 * E // 2)
            for b in range(B):
                for i in range(2):
                    src = back[i * T + b * S:i * T + (b + 1) * S, :].rearrange("(t p) d -> p t d", p=P)
                    sp.dma_start(y01[:, b, i], src).then_inc((y0_in, y1_in)[i][b], 16)
            sp.wait_ge(stored, 16 * B)

        @block.gpsimd
        def _(gp):
            gp.memset(zero[:], 0.0).then_inc(zeroed, 1)
            gp.memset(mhalf[:], -0.5).then_inc(zeroed, 1)
            gp.memset(ones[:], 1.0).then_inc(zeroed, 1)
            gp.memset(base[:], 0.0).then_inc(zeroed, 1)
            for t in (xT_hi, xT_lo):
                for i in range(2):
                    gp.memset(t[:, i, 0:HALF], 0.0).then_inc(zeroed, 1)
                    gp.memset(t[:, i, HALF + S:SP], 0.0).then_inc(zeroed, 1)
            for i in range(2):
                gp.memset(k3[:, i, :, 0:HALF], 0.0).then_inc(zeroed, 1)
                gp.memset(k3[:, i, :, HALF + S:SP], 0.0).then_inc(zeroed, 1)
            gp.memset(vx_lo[:], 0.0).then_inc(zeroed, 1)
            gp.memset(vx_hi[:], 0.0).then_inc(gp_chain, 1)
            gp.wait_ge(gp_chain, 1)
            gp.memset(vx_hi[0:64, :, :, 64:65], 1.0).then_inc(zeroed, 1)
            gp.memset(vx_hi[64:128, :, :, 65:66], 1.0).then_inc(zeroed, 1)
            gp.wait_ge(f32c_in, 16)
            gp.wait_ge(half_in, 16)
            gp.wait_ge(zeroed, 19)
            for i in range(2):
                gp.tensor_scalar(mT[64:96, i, :], half[64:96, 2 * P:3 * P], 1.0, 0.0, ALU.mult, ALU.add).then_inc(mT_rows, 1)
            gp.wait_ge(mT_rows, 2)
            gp.tensor_scalar(x2a[:, :, D + 1], small[:, SM_TOK:SM_TOK + NT], 1.0, 0.0, ALU.mult, ALU.add).then_inc(return_rows, 1)
            gp.tensor_scalar(x2b[:, :, D + 1], small[:, SM_TOK:SM_TOK + NT], float(T), 1.0, ALU.add,
                             ALU.mult).then_inc(return_rows, 1)

            def w_split_third(n):
                e, part = divmod(n, 3)
                cols = slice(part * H, (part + 1) * H)
                gp.wait_ge(w_hi_done, n + 1)
                gp.tensor_tensor(w_lo[:, e, cols], w_raw[:, e, cols], w_hi[:, e, cols].bitcast(F32),
                                 ALU.subtract).then_inc(w_split_gp, 1)

            def o_low(n):
                j = n % 4
                gp.wait_ge(o_hi_done, n + 1)
                gp.tensor_tensor(o_lo[:, j].rearrange("p s (g c) -> p s g c", g=NG),
                                 o32[:, n % 2, :].rearrange("p (g s c) -> p s g c", g=NG, s=2),
                                 o_hi[:, j].rearrange("p s (g c) -> p s g c", g=NG),
                                 ALU.subtract).then_inc(o_lo_done, 1)

            steps = [1]

            def link(ins):
                steps[0] += 1
                ins.then_inc(gp_chain, 1)
                gp.wait_ge(gp_chain, steps[0])

            def expand(u, half):
                expand_wait(gp, u, half)
                for h in HEADS[half]["gp"]:
                    src, dst = expand_aps(u, half, h)
                    gp.tensor_scalar(dst, src, small[0:KR, SM_ROW + h:SM_ROW + h + 1], 1.0, ALU.mult, ALU.mult).then_inc(qx_gp, 1)

            def table(at, i):
                first, n = GROUPS[i]
                return small[:, at:at + 2 * NT].rearrange("p (k t) -> p k t", k=2)[:, :, first:first + n]

            def prepare_indices(i):
                n = GROUPS[i][1]
                f = flat[:, :, 0:n]
                gp.wait_ge(label_done, i + 1)
                link(gp.tensor_scalar(f, pos[:, :, 0:n], -float(CAP), float(E * CAP), ALU.mult, ALU.add))
                link(gp.tensor_tensor(f, f, table(SM_FLAT, i), ALU.subtract))

            def send_indices(i):
                first, n = GROUPS[i]
                f, v, sl, ix = flat[:, :, 0:n], valid[:, :, 0:n], slot[:, :, 0:n], index[:, :, first:first + n]
                gp.wait_ge(slot_done, i + 1)
                gp.tensor_tensor(f, f, sl, ALU.add).then_inc(gp_chain, 1)
                steps[0] += 1
                link(gp.tensor_scalar(v, sl, float(CAP), 1.0, ALU.is_le, ALU.mult))
                link(gp.tensor_tensor(f, f, v, ALU.mult))
                link(gp.tensor_tensor(f, f, table(SM_DUMP, i), ALU.add))
                gp.tensor_copy(ix, f).then_inc(index_done, 1)
                gp.wait_ge(index_done, i + 1)
                gp.wait_ge(rows_done, i + 1)
                gp.wait_ge(x2b_done, i + 1)
                if i == 0:
                    gp.wait_ge(dram_set, 32)

            def send(i, t, k):
                first = GROUPS[i][0]
                tile = first + t
                gp.indirect_dma_start(
                    disp, bass.IndirectOffsetOnAxis(ap=index[:, k, tile:tile + 1], axis=0),
                    (x2a, x2b)[k][:, tile, :], None).then_inc(sent[i], 16)

            def add_bias(b):
                gp.wait_ge(spare_filled, count("xT", b))
                xb = x_sb[:, b * TR:(b + 1) * TR, :]
                gp.tensor_tensor(xb, xb, rows[:, 0:D].unsqueeze(1).to_broadcast([P, TR, D]), ALU.add).then_inc(bo_added, 1)

            expand(0, 0)
            expand(0, 1)
            gp.wait_ge(rows_in, 16)
            add_bias(0)
            to_send = []
            for s in range(STEPS):
                if s - LAG_P in LOW_P_GP:
                    low_p(gp, s - LAG_P)
                if 0 <= s - LAG_H < SPU * NU:
                    o_low(s - LAG_H)
                for what, i in after_step(s - 1):
                    if what == "WO":
                        gp.wait_ge(var_done, i + 1)
                        gp.tensor_tensor(rstd[:, 0:2], vareps[:, 0:2], mhalf[:, 0:2], ALU.pow).then_inc(rstd_done, 1)
                    if what == "q":
                        add_bias(i)
                for what, i in after_step(s - 2):
                    if what == "LG":
                        prepare_indices(i)
                for what, i in after_step(s - (2 if s < SPU * NU else 1)):
                    if what == "RK":
                        send_indices(i)
                        to_send += [(i, t, k) for t in range(GROUPS[i][1]) for k in range(2)]
                if s < SPU * (NU - 1) and s % SPU >= 2:
                    expand(s // SPU + 1, s % SPU - 2)
                now = 1 if s < SPU * NU else 2 if s < SPU * (NU + 1) else SENDS_LAST[min(s - SPU * (NU + 1), 4)]
                for rows_of in to_send[:now]:
                    send(*rows_of)
                to_send = to_send[now:]

            for n in range(SPLIT_VE, 3 * E):
                w_split_third(n)

            for e in range(E):
                gp.wait_ge(ye_done, 3 * (e + 1))
                gp.wait_ge(ret_done, 2 * (e + 1))
                for j in range(3):
                    n = P if j < 2 else 64
                    gp.indirect_dma_start(
                        back, bass.IndirectOffsetOnAxis(ap=ret[0:n, e % 4, j:j + 1], axis=0),
                        ye[0:n, e % 2, j, :], None).then_inc(returned[e % 2], 16)
            for b in range(B + 2):
                if b < B:
                    gp.wait_ge(y0_in[b], 16)
                    gp.tensor_tensor(y01[:, b, 0], y01[:, b, 0], x2a[:, b * TR:(b + 1) * TR, 0:D], ALU.add).then_inc(y_sum, 1)
                if b >= 2:
                    gp.wait_ge(fin_var, b - 1)
                    gp.tensor_tensor(frstd[:, b - 2, :], fvar[:, b - 2, :], mhalf[:], ALU.pow).then_inc(fin_rstd, 1)

        @block.scalar
        def _(act):
            def o_high(n):
                act.wait_ge(o32_done, n + 1)
                if n % 4 == 0 and n >= 4:
                    act.wait_ge(spare_filled, count("AT", n // 4 - 1))
                act.activation(o_hi[:, n % 4].rearrange("p s (g c) -> p s g c", g=NG),
                               o32[:, n % 2, :].rearrange("p (g s c) -> p s g c", g=NG, s=2), ACT.Copy).then_inc(o_hi_done, 1)

            def prepare(what, i):
                if what == "xT":
                    act.wait_ge(spare_filled, count(what, i))
                    act.activation(xT_hi[:, i % 2, HALF:HALF + S], mb((what, i))[:, :], ACT.Copy).then_inc(xT_hi_done, 1)
                if what in "qk":
                    c = "qk".index(what)
                    act.wait_ge(spare_filled, count(what, i))
                    if i >= 1:
                        act.wait_ge(parts_out[c][0], 16 * i)
                    act.activation(qk_hi[:, c, :], mb((what, i))[:, :], ACT.Identity,
                                   bias=bias[:, c:c + 1]).then_inc(qk_hi_done, 1)
                if what == "V":
                    act.wait_ge(spare_filled, count(what, i))
                    act.wait_ge(zeroed, 19)
                    v = mb((what, i))[:, :].rearrange("p (a c) -> p a c", c=32)
                    act.activation(vx_hi[0:64, i % 2, :, 0:32], v[0:64], ACT.Copy).then_inc(vx_hi_done, 1)
                    act.activation(vx_hi[64:128, i % 2, :, 32:64], v[64:128], ACT.Copy).then_inc(vx_hi_done, 1)

            def w_high(n):
                e, part = divmod(n, 3)
                cols = slice(part * H, (part + 1) * H)
                act.wait_ge(w_in[n], 16)
                act.activation(w_hi[:, e, cols], w_raw[:, e, cols], ACT.Copy).then_inc(w_hi_done, 1)

            def expand(u, half):
                expand_wait(act, u, half)
                for h in HEADS[half]["act"]:
                    src, dst = expand_aps(u, half, h)
                    act.activation(dst, src, ACT.Copy, scale=small[0:KR, SM_ROW + h:SM_ROW + h + 1]).then_inc(qx_act, 1)

            act.wait_ge(wp_in, 16)
            act.activation(wp_hi[:].rearrange("p a b -> p (a b)"), w_proj_sb[:, 0:4 * D], ACT.Copy).then_inc(wp_split_hi, 1)
            act.wait_ge(f32c_in, 16)
            for what in ("xT", "q", "k"):
                prepare(what, 0)
            expand(0, 0)
            expand(0, 1)
            for s in range(STEPS):
                n = s - LAG_P
                if 0 <= n < SPU * NU:
                    act.wait_ge(t_filled, n + 1)
                    if n >= 2:
                        act.wait_ge(p_lo_done[n % 2], n // 2)
                        act.wait_ge(o_filled, n - 1)
                    act.activation(p32[:, n % 2, :], t_bank[n % 2][:, :], ACT.Exp, scale=SCALE).then_inc(p32_done, 1)
                    act.activation(p_hi[:, n % 2, :], t_bank[n % 2][:, :], ACT.Exp, scale=SCALE).then_inc(p_hi_done, 1)
                if 0 <= s - LAG_H < SPU * NU:
                    o_high(s - LAG_H)
                for what, i in after_step(s - 1):
                    if what in ("xT", "q", "k", "V"):
                        prepare(what, i)
                    if what == "AT":
                        act.wait_ge(spare_filled, count(what, i))
                        act.activation(at_hi[:], mb((what, i))[:, 0:UT], ACT.Identity, bias=bias[:, 2:3]).then_inc(at_hi_done, 1)
                    if what == "XT2":
                        first, n = GROUPS[i]
                        act.wait_ge(x2_done, first + n)
                        act.activation(x2b[:, first:first + n, 0:D], x2a[:, first:first + n, 0:D], ACT.Copy).then_inc(x2b_done, 1)
                if split_in(s) is not None:
                    w_high(split_in(s))
                if s < SPU * (NU - 1) and s % SPU >= 2:
                    expand(s // SPU + 1, s % SPU - 2)
                for what, i in after_step(s - 2):
                    if what == "LG":
                        act.wait_ge(gap_done, i + 1)
                        n = GROUPS[i][1]
                        act.activation(egap[:, 0:n], gap[:, 0:n], ACT.Exp).then_inc(egap_done, 1)

            for n in range(SPLIT_ACT, 3 * E):
                w_high(n)

            act.activation(rstd[:, 2:3], mhalf[:, 0:1], ACT.Silu).then_inc(silu_set, 1)

            def expert_in(e):
                act.wait_ge(xeT_filled, e + 1)
                act.activation(xeT_hi[:, e % 2, :], m_bank[0][:, 0:CAP], ACT.Copy).then_inc(xeT_hi_done, 1)

            def expert_out(e):
                act.wait_ge(w3_done, HC * (e + 1))
                if e >= 2:
                    act.wait_ge(yb_filled, e - 1)
                act.activation(yT[:, e % 2, :], o_bank[e % 2][:, 0:CAP], ACT.Copy).then_inc(yT_done, 1)

            expert_in(0)
            for m in range(HC * E + LAG + 1):
                if m < HC * E:
                    act.wait_ge(ab_filled, m + 1)
                    if m >= 2:
                        act.wait_ge(h_done, m - 1)
                    act.activation(gate[:, m % 2, :], s_bank[m % 2][:, 0:CAP], ACT.Silu).then_inc(gate_done, 1)
                if 1 <= m <= HC * E:
                    k = m - 1
                    act.wait_ge(h_done, k + 1)
                    if k >= 4:
                        act.wait_ge(w3_done, k - 3)
                    act.activation(h_hi[:, k % 4, :], h32[:, k % 2, :], ACT.Copy).then_inc(h_hi_done, 1)
                if m % HC == 1 and m // HC + 1 < E:
                    expert_in(m // HC + 1)
                if m % HC == (HC - 1 + LAG) % HC and m >= HC - 1 + LAG:
                    expert_out((m - (HC - 1 + LAG)) // HC)
            for b in range(B):
                act.wait_ge(fin_shift, b + 1)
                for t in range(TR if b < B - 1 else TR // 2):
                    act.activation(zo[:, b, t, :], z[:, b, t, :], ACT.Identity, bias=fshift[:, b, t:t + 1],
                                   scale=frstd[:, b, t:t + 1]).then_inc(fin_done, 1)
                act.wait_ge(fin_done, TR * (b + 1) if b < B - 1 else TR * b + TR // 2)
                if b == B - 1:
                    act.wait_ge(last_done, TR - TR // 2)
                act.dma_start(out_d[b], zo[:, b]).then_inc(stored, 16)

        @block.vector
        def _(ve):
            steps = [0]

            def link(ins):
                steps[0] += 1
                ins.then_inc(chain, 1)
                ve.wait_ge(chain, steps[0])

            def link_all(all_ins):
                for ins in all_ins:
                    steps[0] += 1
                    ins.then_inc(chain, 1)
                ve.wait_ge(chain, steps[0])

            ve.wait_ge(wp_split_hi, 1)
            ve.tensor_tensor(wp_lo[:].rearrange("p a b -> p (a b)"), w_proj_sb[:, 0:4 * D],
                             wp_hi[:].rearrange("p a b -> p (a b)"), ALU.subtract).then_inc(wp_split, 1)
            ve.wait_ge(f32c_in, 16)

            def prepare(what, i):
                if what == "xT":
                    ve.wait_ge(xT_hi_done, i + 1)
                    ve.tensor_tensor(xT_lo[:, i % 2, HALF:HALF + S], mb((what, i))[:, :],
                                     xT_hi[:, i % 2, HALF:HALF + S], ALU.subtract).then_inc(spare_free, 1)
                if what in "qk":
                    c = "qk".index(what)
                    ve.wait_ge(qk_hi_done, 2 * i + c + 1)
                    if i >= 1:
                        ve.wait_ge(parts_out[c][1], 16 * i)
                    ve.scalar_tensor_tensor(out=qk_lo[:, c, :], in0=mb((what, i))[:, :], scalar=bias[:, c:c + 1],
                                            in1=qk_hi[:, c, :], op0=ALU.add, op1=ALU.subtract).then_inc(spare_free, 1)
                if what == "V":
                    v = mb((what, i))[:, :].rearrange("p (a c) -> p a c", c=32)
                    ve.wait_ge(vx_hi_done, 2 * i + 2)
                    for k in range(2):
                        rows_, cols = slice(64 * k, 64 * k + 64), slice(32 * k, 32 * k + 32)
                        ins = ve.tensor_tensor(vx_lo[rows_, i % 2, :, cols], v[rows_], vx_hi[rows_, i % 2, :, cols], ALU.subtract)
                    ins.then_inc(spare_free, 1)

            def expand(u, half):
                expand_wait(ve, u, half)
                for h in HEADS[half]["ve"]:
                    src, dst = expand_aps(u, half, h)
                    ve.tensor_scalar(dst, src, small[0:KR, SM_ROW + h:SM_ROW + h + 1], None, ALU.mult).then_inc(qx_ve, 1)

            def reciprocals(n):
                ve.wait_ge(o_filled, n + 1)
                o = o_bank[n % 2][:, 0:NG * OC].rearrange("p (g c) -> p g c", g=NG)
                steps[0] += 1
                ve.reciprocal(rden[:], o[:, :, 64:66]).then_inc(chain, 1)

            def mask_heads(n):
                ve.wait_ge(chain, steps[0])
                steps[0] += 1
                ve.tensor_tensor(rmask[:], rden[:].unsqueeze(3).to_broadcast([P, NG, 2, HG]),
                                 small[:, SM_HEAD:SM_HEAD + HG].unsqueeze(1).unsqueeze(1).to_broadcast([P, NG, 2, HG]),
                                 ALU.mult).then_inc(chain, 1)

            def normalise(n):
                ve.wait_ge(chain, steps[0])
                o = o_bank[n % 2][:, 0:NG * OC].rearrange("p (g c) -> p g c", g=NG)
                if n >= 2:
                    ve.wait_ge(o_lo_done, n - 1)
                ve.tensor_tensor(o32[:, n % 2, :].rearrange("p (g a c) -> p g a c", g=NG, a=8),
                                 o[:, :, 0:64].rearrange("p g (a c) -> p g a c", a=8),
                                 rmask[:].rearrange("p g s h -> p g (s h)").unsqueeze(3).to_broadcast([P, NG, 8, HD]),
                                 ALU.mult).then_inc(o32_done, 1)

            def route(i):
                n = GROUPS[i][1]
                g, w = lg[:, 0:n], tmp[:, :, 0:n]
                both = [P, 2, n, E]
                ve.wait_ge(spare_filled, count("LG", i))
                if i == 0:
                    ve.wait_ge(rows_in, 16)
                if i >= 1:
                    ve.wait_ge(index_done, i)
                    ve.wait_ge(egap_done, i)
                ve.tensor_tensor(g, mb(("LG", i))[:, 0:n * E].rearrange("p (t e) -> p t e", e=E),
                                 rows[:, D:D + E].unsqueeze(1).to_broadcast([P, n, E]), ALU.add).then_inc(spare_free, 1)
                ve.wait_ge(spare_free, count("LG", i))
                rev = small[:, SM_REV:SM_REV + E].unsqueeze(1)
                link_all([ve.max(top[:, t, :], lg[:, t, :]) for t in range(n)])
                ve.tensor_tensor(gap[:, 0:n], top[:, 0:n, 1], top[:, 0:n, 0], ALU.subtract).then_inc(gap_done, 1)
                link(ve.tensor_tensor(w, g.unsqueeze(1).to_broadcast(both),
                                      top[:, 0:n, 0:2].rearrange("p t k -> p k t").unsqueeze(3).to_broadcast(both), ALU.is_equal))
                link(ve.tensor_tensor(w, w, rev.unsqueeze(1).to_broadcast(both), ALU.mult))
                for k in range(2):
                    link(ve.tensor_reduce(pos[:, k, 0:n], w[:, k], AX, ALU.max))
                    link(ve.tensor_tensor(pick[:, k, 0:n], pos[:, k, 0:n].unsqueeze(2).to_broadcast([P, n, E]),
                                          rev.to_broadcast([P, n, E]), ALU.is_equal))
                    if k == 0:
                        link(ve.scalar_tensor_tensor(out=w[:, 1], in0=pick[:, 0, 0:n], scalar=-2.0 * E, in1=w[:, 1],
                                                     op0=ALU.mult, op1=ALU.add))
                ve.tensor_tensor(label[:, 0:n], pick[:, 0, 0:n], pick[:, 1, 0:n], ALU.add).then_inc(label_done, 1)

            def place(i):
                first, n = GROUPS[i]
                w = tmp[:, :, 0:n]
                ve.wait_ge(spare_filled, count("RK", i))
                m = mb(("RK", i))
                link(ve.tensor_tensor(seq[:, 0:n], m[:, 0:n * E].rearrange("p (t e) -> p t e", e=E),
                                      base[:].unsqueeze(1).to_broadcast([P, n, E]), ALU.add))
                ve.tensor_tensor(base[:], m[:, TR * E:TR * E + E], base[:], ALU.add).then_inc(spare_free, 1)
                link(ve.tensor_tensor(w, seq[:, 0:n].unsqueeze(1).to_broadcast([P, 2, n, E]), pick[:, :, 0:n], ALU.mult))
                ve.tensor_reduce(slot[:, :, 0:n], w, AX, ALU.add).then_inc(slot_done, 1)
                ve.wait_ge(egap_done, i + 1)
                if i == 0:
                    ve.wait_ge(return_rows, 2)
                ve.wait_ge(x2b_done, i + 1)
                link(ve.tensor_scalar(wgt[:, 0, 0:n], egap[:, 0:n], 1.0, None, ALU.add))
                xa, xb = x2a[:, first:first + n, D], x2b[:, first:first + n, D]
                link(ve.reciprocal(xa, wgt[:, 0, 0:n]))
                ve.tensor_tensor(xb, xa, egap[:, 0:n], ALU.mult).then_inc(rows_done, 1)

            for what in ("xT", "q", "k"):
                prepare(what, 0)
            expand(0, 0)
            expand(0, 1)
            for s in range(STEPS):
                u, j = divmod(s, SPU)
                if j == 0 and 1 <= u <= NU:
                    ve.wait_ge(spare_filled, count("mT", u - 1))
                    ve.tensor_copy(mT[0:64, (u - 1) % 2, :], mb(("mT", u - 1))[0:64, 0:64].bitcast(BF16)).then_inc(spare_free, 1)
                if u < NU:
                    ve.wait_ge(s_filled, s + 1)
                    ve.tensor_reduce(nmax[:, u % 2, 8 * j:8 * j + 8], s_bank[s % 2][:, :].rearrange("p (a k) -> p a k", k=KW),
                                     AX, ALU.max, negate=True).then_inc(s_maxed, 1)
                    if j == SPU - 1:
                        ve.wait_ge(s_maxed, s + 1)
                        ve.tensor_copy(nmax2[:, 0, :], nmax[:, u % 2, :]).then_inc(nmax_hi, 1)
                        ve.wait_ge(nmax_hi, u + 1)
                        ve.tensor_tensor(nmax2[:, 1, :], nmax[:, u % 2, :], nmax2[:, 0, :], ALU.subtract).then_inc(nmax_split, 1)
                for what, i in after_step(s - 1):
                    if what in ("xT", "q", "k", "V"):
                        prepare(what, i)
                    if what == "AT":
                        ve.wait_ge(at_hi_done, i + 1)
                        ve.scalar_tensor_tensor(out=at_lo[:], in0=mb((what, i))[:, 0:UT], scalar=bias[:, 2:3],
                                                in1=at_hi[:], op0=ALU.add, op1=ALU.subtract).then_inc(spare_free, 1)
                    if what == "WO":
                        ve.wait_ge(spare_filled, count(what, i))
                        ve.wait_ge(bo_added, i // 2 + 1)
                        ve.tensor_tensor(res[:], mb((what, i))[:, 0:UT].rearrange("p (t d) -> p t d", t=2),
                                         x_sb[:, 2 * i:2 * i + 2, :], ALU.add).then_inc(spare_free, 1)
                        ve.wait_ge(spare_free, count(what, i))
                        link_all([ve.bn_stats(stats[:, t, :], res[:, t, :]) for t in range(2)])
                        link_all([ve.bn_aggr(mv[:, t, :], stats[:, t, :]) for t in range(2)])
                        ve.tensor_scalar(vareps[:, 0:2], mv[:, 0:2, 1], EPS, None, ALU.add).then_inc(var_done, 1)
                    if what == "XT2":
                        ve.wait_ge(spare_filled, count(what, i))
                        cols = GROUPS[i][1] * P
                        ve.tensor_copy(x2T[:, 0:cols], mb((what, i))[:, 0:cols]).then_inc(spare_free, 1)
                if 0 <= s - LAG_O < SPU * NU:
                    reciprocals(s - LAG_O)
                if 0 <= s - LAG_P < SPU * NU and s - LAG_P not in LOW_P_GP:
                    low_p(ve, s - LAG_P)
                if 0 <= s - LAG_O < SPU * NU:
                    mask_heads(s - LAG_O)
                if s < SPU * (NU - 1) and j >= 2:
                    expand(u + 1, j - 2)
                if 0 <= s - LAG_O < SPU * NU:
                    normalise(s - LAG_O)
                for what, i in after_step(s - 1):
                    if what == "WO":
                        ve.wait_ge(rstd_done, i + 1)
                        for t in range(2):
                            ve.tensor_scalar(x2a[:, 2 * i + t, 0:D], res[:, t, :], mv[:, t, 0:1], rstd[:, t:t + 1],
                                             ALU.subtract, ALU.mult).then_inc(x2_done, 1)
                    if what == "LG":
                        route(i)
                    if what == "RK":
                        place(i)

            for n in range(SPLIT_VE):
                e, part = divmod(n, 3)
                cols = slice(part * H, (part + 1) * H)
                ve.wait_ge(w_hi_done, n + 1)
                ve.tensor_tensor(w_lo[:, e, cols], w_raw[:, e, cols], w_hi[:, e, cols].bitcast(F32),
                                 ALU.subtract).then_inc(w_split_ve, 1)

            def expert_in(e):
                ve.wait_ge(xeT_hi_done, e + 1)
                ve.tensor_tensor(xeT_lo[:, e % 2, :], m_bank[0][:, 0:CAP], xeT_hi[:, e % 2, :].bitcast(F32),
                                 ALU.subtract).then_inc(xeT_split, 1)
                if e >= 4:
                    ve.wait_ge(returned[e % 2], 48 * ((e - 4) // 2 + 1))
                ve.wait_ge(xe_in[e % 4], 32 * (e // 4 + 1))
                ve.tensor_copy(ret[:, e % 4, 0:2], xe[:, e % 4, 0:2, D + 1]).then_inc(ret_done, 1)
                ve.tensor_copy(ret[0:64, e % 4, 2:3], xe[0:64, e % 4, 2, D + 1:D + 2]).then_inc(ret_done, 1)

            def expert_back(e):
                ve.wait_ge(yb_filled, e + 1)
                if e >= 2:
                    ve.wait_ge(returned[e % 2], 48 * (e // 2))
                for j in range(3):
                    n = P if j < 2 else 64
                    ve.tensor_scalar(ye[0:n, e % 2, j, :], m_bank[1][0:n, j * D:(j + 1) * D], xe[0:n, e % 4, j, D:D + 1],
                                     None, ALU.mult).then_inc(ye_done, 1)

            expert_in(0)
            for m in range(HC * E + LAG + 1):
                if m < HC * E:
                    ve.wait_ge(gate_done, m + 1)
                    if m >= 2:
                        ve.wait_ge(h_hi_done, m - 1)
                        ve.wait_ge(h_split, m - 1)
                    ve.tensor_tensor(h32[:, m % 2, :], gate[:, m % 2, :], t_bank[m % 2][:, 0:CAP], ALU.mult).then_inc(h_done, 1)
                if 1 <= m <= HC * E:
                    k = m - 1
                    ve.wait_ge(h_hi_done, k + 1)
                    if k >= 4:
                        ve.wait_ge(w3_done, k - 3)
                    ve.tensor_tensor(h_lo[:, k % 4, :], h32[:, k % 2, :], h_hi[:, k % 4, :].bitcast(F32),
                                     ALU.subtract).then_inc(h_split, 1)
                if m % HC == 1 and m // HC + 1 < E:
                    expert_in(m // HC + 1)
                if m % HC == (HC + LAG) % HC and m >= HC + LAG:
                    expert_back((m - HC - LAG) // HC)
            for b in range(B + 1):
                if b < B:
                    ve.wait_ge(y_sum, b + 1)
                    ve.wait_ge(y1_in[b], 16)
                    link(ve.tensor_tensor(z[:, b], y01[:, b, 0], y01[:, b, 1], ALU.add))
                    link_all([ve.bn_stats(stats[:, t, :], z[:, b, t, :]) for t in range(TR)])
                    link_all([ve.bn_aggr(fmv[:, b, t, :], stats[:, t, :]) for t in range(TR)])
                    ve.tensor_scalar(fvar[:, b, :], fmv[:, b, :, 1], EPS, None, ALU.add).then_inc(fin_var, 1)
                if b >= 1:
                    ve.wait_ge(fin_rstd, b)
                    ve.scalar_tensor_tensor(out=fshift[:, b - 1, :], in0=fmv[:, b - 1, :, 0], scalar=-1.0,
                                            in1=frstd[:, b - 1, :], op0=ALU.mult, op1=ALU.mult).then_inc(fin_shift, 1)
            for t in range(TR // 2, TR):
                ve.tensor_scalar(zo[:, B - 1, t, :], z[:, B - 1, t, :], fmv[:, B - 1, t, 0:1], frstd[:, B - 1, t:t + 1],
                                 ALU.subtract, ALU.mult).then_inc(last_done, 1)

        @block.tensor
        def _(pe):
            def spare_bank(use):
                if spare[use] >= 2:
                    pe.wait_ge(spare_free, spare[use] - 1)
                return mb(use)

            def scores_q(n):
                u, j = divmod(n, 4)
                if n >= 2:
                    pe.wait_ge(s_maxed, n - 1)
                if j % 2 == 0:
                    for done, at in expanded(u, j // 2):
                        pe.wait_ge(done, at)
                if j == 0:
                    pe.wait_ge(k3_in, 16 * NTERM * (u // 2 + 1))
                bank, b, blk = s_bank[n % 2], u // 2, (u % 2) * UB + 2 * j
                pe.matmul(bank[:, :].rearrange("p (s g k) -> p s g k", s=2, g=NG), onehot,
                          mask[:, blk:blk + 2, :].unsqueeze(2).to_broadcast([QB, 2, NG, KW]),
                          start=True, stop=False, skip_group_check=True)
                for s in range(2):
                    for g in range(NG):
                        c = (s * NG + g) * KW
                        mm = pe.matmul(bank[:, c:c + KW], qx[:, u % 2, g, 2 * j + s, :],
                                       k3[:, b % 2, g, QB * (blk + s):QB * (blk + s) + KW],
                                       start=False, stop=True, skip_group_check=True)
                mm.then_inc(s_filled, 1)

            def scores_k(n):
                u, j = divmod(n, 4)
                b, half = divmod(u, 2)
                if j == 0:
                    pe.wait_ge(spare_free, count("mT", u))
                if n >= 2:
                    pe.wait_ge(p_hi_done, n - 1)
                bank = t_bank[n % 2]
                for g in range(NG):
                    pe.matmul(bank[:, g * P:(g + 1) * P], aux[:, half, j, g, :], mT[:, u % 2, :],
                              start=(g == 0), stop=False, skip_group_check=True)
                for s, blk in enumerate(PAIRS[j]):
                    key = QB * (half * UB + blk)
                    for g in range(NG):
                        mm = pe.matmul(bank[KW * s:KW * s + KW, g * P:(g + 1) * P],
                                       k3[:, b % 2, g, key:key + KW], qx[:, u % 2, g, blk, :],
                                       start=False, stop=True, skip_group_check=True)
                mm.then_inc(t_filled, 1)

            def output(n):
                u, j = divmod(n, 4)
                pe.wait_ge(p_lo_done[n % 2], n // 2 + 1)
                if j == 0:
                    pe.wait_ge(spare_free, count("V", u))
                if n >= 2:
                    pe.wait_ge(o32_done, n - 1)
                for g in range(NG):
                    o = o_bank[n % 2][:, g * OC:(g + 1) * OC]
                    hi, lo = p_hi[:, n % 2, g * P:(g + 1) * P], p_lo[:, n % 2, g * P:(g + 1) * P]
                    vh, vl = vx_hi[:, u % 2, j * NG + g, :], vx_lo[:, u % 2, j * NG + g, :]
                    pe.matmul(o, hi, vh, start=True, stop=False)
                    pe.matmul(o, hi, vl, start=False, stop=False)
                    mm = pe.matmul(o, lo, vh, start=False, stop=True)
                mm.then_inc(o_filled, 1)

            def prepare(what, i):
                m = spare_bank((what, i))
                if what == "xT":
                    pe.wait_ge(x_in[i], 16)
                    for t in range(TR):
                        mm = pe.transpose(m[:, t * P:(t + 1) * P], x_sb[:, i * TR + t, :], ident)
                if what in "qk":
                    if what == "q":
                        pe.wait_ge(xT_hi_done, i + 1)
                        pe.wait_ge(wp_split, 1)
                    c = "qk".index(what)
                    xh, xl = (t[:, i % 2, HALF:HALF + S] for t in (xT_hi, xT_lo))
                    pe.matmul(m[:, :], wp_hi[:, c, :], xh, start=True, stop=False)
                    pe.matmul(m[:, :], wp_lo[:, c, :], xh, start=False, stop=False)
                    if what == "q":
                        pe.wait_ge(spare_free, count("xT", i))
                    mm = pe.matmul(m[:, :], wp_hi[:, c, :], xl, start=False, stop=True)
                if what == "V":
                    for k, (first, _) in enumerate(PAIRS):
                        key = QB * ((i % 2) * UB + first)
                        xh, xl = (t[:, i // 2 % 2, key:key + P] for t in (xT_hi, xT_lo))
                        o = m[:, k * D:(k + 1) * D]
                        pe.matmul(o, xh, wp_hi[:, 2, :], start=True, stop=False)
                        pe.matmul(o, xh, wp_lo[:, 2, :], start=False, stop=False)
                        mm = pe.matmul(o, xl, wp_hi[:, 2, :], start=False, stop=True)
                mm.then_inc(spare_filled, 1)

            pe.wait_ge(f32c_in, 16)
            for what in ("xT", "q", "k"):
                prepare(what, 0)
            pe.wait_ge(half_in, 16)
            pe.wait_ge(zeroed, 19)
            scores_q(0)
            for s in range(STEPS):
                if 0 <= s - LAG_O < SPU * NU:
                    output(s - LAG_O)
                if s % SPU == 0 and s + 1 < SPU * NU:
                    scores_q(s + 1)
                if 0 <= s - LAG_K < SPU * NU:
                    if s == LAG_K:
                        pe.wait_ge(aux_in, 16)
                        pe.wait_ge(mT_rows, 2)
                    scores_k(s - LAG_K)
                if s % SPU and s + 1 < SPU * NU:
                    scores_q(s + 1)
                for what, i in after_step(s):
                    if what not in PSUM_USES:
                        continue
                    if what in ("xT", "q", "k", "V"):
                        prepare(what, i)
                        continue
                    m = spare_bank((what, i))
                    first, n = GROUPS[i] if what in ("XT2", "LG", "RK") else (0, 0)
                    if what == "mT":
                        pe.wait_ge(nmax_split, i + 1)
                        mm = pe.transpose(m[0:64, 0:64].bitcast(BF16), nmax2[:].rearrange("p s c -> p (s c)"), identb)
                    if what == "AT":
                        pe.wait_ge(o_lo_done, 4 * i + 4)
                        for k, pair in enumerate(PAIRS):
                            for half_, blk in enumerate(pair):
                                o = m[:, blk * QB:(blk + 1) * QB]
                                pe.matmul(o, o_hi[:, k, half_, :], merge, start=True, stop=False)
                                mm = pe.matmul(o, o_lo[:, k, half_, :], merge, start=False, stop=True)
                    if what == "WO":
                        pe.wait_ge(spare_free, count("AT", i))
                        for t in range(2):
                            o, ah, al = m[:, t * D:(t + 1) * D], at_hi[:, t * P:(t + 1) * P], at_lo[:, t * P:(t + 1) * P]
                            pe.matmul(o, ah, wp_hi[:, 3, :], start=True, stop=False)
                            pe.matmul(o, ah, wp_lo[:, 3, :], start=False, stop=False)
                            mm = pe.matmul(o, al, wp_hi[:, 3, :], start=False, stop=True)
                    if what == "XT2":
                        pe.wait_ge(x2_done, first + n)
                        for t in range(n):
                            mm = pe.transpose(m[:, t * P:(t + 1) * P], x2a[:, first + t, 0:D], ident)
                    if what == "LG":
                        pe.wait_ge(spare_free, count("XT2", i))
                        for t in range(n):
                            mm = pe.matmul(m[:, t * E:(t + 1) * E], x2T[:, t * P:(t + 1) * P], wg, start=True, stop=True)
                    if what == "RK":
                        pe.wait_ge(label_done, i + 1)
                        for t in range(n):
                            o = m[:, t * E:(t + 1) * E]
                            for before in range(t + 1):
                                pe.matmul(o, tri if before == t else ones[:], label[:, before, :],
                                          start=(before == 0), stop=(before == t))
                        for t in range(n):
                            mm = pe.matmul(m[:, TR * E:(TR + 1) * E], ones[:], label[:, t, :], start=(t == 0), stop=(t == n - 1))
                    mm.then_inc(spare_filled, 1)

            def expert_in(e):
                pe.wait_ge(xe_in[e % 4], 32 * (e // 4 + 1))
                if e == 0:
                    pe.wait_ge(spare_free, len(spare))
                if e >= 1:
                    pe.wait_ge(xeT_split, e)
                for j in range(3):
                    n = P if j < 2 else 64
                    mm = pe.transpose(m_bank[0][:, j * P:j * P + n], xe[0:n, e % 4, j, 0:D], f32c[0:n, 0:n])
                mm.then_inc(xeT_filled, 1)

            def up(m):
                e, c = divmod(m, HC)
                if c == 0:
                    pe.wait_ge(xeT_split, e + 1)
                    pe.wait_ge(w_split_ve, min(3 * (e + 1), SPLIT_VE))
                    if 3 * (e + 1) > SPLIT_VE:
                        pe.wait_ge(w_split_gp, 3 * (e + 1) - SPLIT_VE)
                if m >= 2:
                    pe.wait_ge(h_done, m - 1)
                xh, xl = xeT_hi[:, e % 2, :], xeT_lo[:, e % 2, :]
                for bank, first in ((s_bank[m % 2], 0), (t_bank[m % 2], H)):
                    cols = slice(first + c * P, first + (c + 1) * P)
                    pe.matmul(bank[:, 0:CAP], w_hi[:, e, cols], xh, start=True, stop=False)
                    pe.matmul(bank[:, 0:CAP], w_hi[:, e, cols], xl, start=False, stop=False)
                    mm = pe.matmul(bank[:, 0:CAP], w_lo[:, e, cols], xh, start=False, stop=True)
                mm.then_inc(ab_filled, 1)

            def down(m):
                e, c = divmod(m, HC)
                pe.wait_ge(h_split, m + 1)
                if c == 0 and e >= 2:
                    pe.wait_ge(yT_done, e - 1)
                cols = slice(2 * H + c * P, 2 * H + (c + 1) * P)
                o = o_bank[e % 2][:, 0:CAP]
                pe.matmul(o, w_hi[:, e, cols], h_hi[:, m % 4, :], start=(c == 0), stop=False)
                pe.matmul(o, w_hi[:, e, cols], h_lo[:, m % 4, :], start=False, stop=False)
                mm = pe.matmul(o, w_lo[:, e, cols], h_hi[:, m % 4, :], start=False, stop=(c == HC - 1))
                mm.then_inc(w3_done, 1)

            def expert_back(e):
                pe.wait_ge(yT_done, e + 1)
                if e >= 1:
                    pe.wait_ge(ye_done, 3 * e)
                for j in range(3):
                    n = P if j < 2 else 64
                    mm = pe.transpose(m_bank[1][0:n, j * D:(j + 1) * D], yT[:, e % 2, j * P:j * P + n], ident)
                mm.then_inc(yb_filled, 1)

            expert_in(0)
            for m in range(HC * E + LAG + 1):
                if m < HC * E:
                    up(m)
                if m % HC == 0 and m // HC + 1 < E:
                    expert_in(m // HC + 1)
                if LAG <= m < HC * E + LAG:
                    down(m - LAG)
                if m % HC == (HC + LAG) % HC and m >= HC + LAG:
                    expert_back((m - HC - LAG) // HC)


PSUM_USES = ("xT", "q", "k", "V", "mT", "AT", "WO", "XT2", "LG", "RK")


def after_step(s):
    u, j = divmod(s, SPU)
    uses = []
    if s < 0:
        return uses
    if u < NU and j == 0 and u % 2 == 0 and u // 2 + 1 < B:
        uses.append(("xT", u // 2 + 1))
    if u < NU and j == 1:
        uses.append(("V", u))
    if 0 <= u - 2 < NU and j == 2:
        uses.append(("AT", u - 2))
    if u < NU and j == SPU - 1:
        uses.append(("mT", u))
    if 0 <= u - 2 < NU and j == SPU - 1:
        uses.append(("WO", u - 2))
    if u < NU and u % 2 == 0 and u // 2 + 1 < B and j in (1, 2):
        uses.append(("qk"[j - 1], u // 2 + 1))
    for step_of, what in enumerate(("XT2", "LG", "RK")):
        for i, (first, n) in enumerate(GROUPS):
            unit = (first + n) // 2 - 1
            late = 1 + (what == "RK") if unit + 3 < NU else unit == NU - 2 and what == "RK"
            if s == SPU * (unit + 3) + step_of + late:
                uses.append((what, i))
    return uses


def split_in(s):
    n = s // SPU
    return n if s % SPU == SPU - 1 and n < SPLIT_ACT else None


def kernel(L0_attn_x, L0_attn_Wq, L0_attn_bq, L0_attn_Wk, L0_attn_bk, L0_attn_Wv, L0_attn_bv, L0_attn_Wo, L0_attn_bo,
           L0_ffn_Wg, L0_ffn_bg, L0_ffn_W1, L0_ffn_W2, L0_ffn_W3):
    import concourse.bacc as bacc
    from concourse.bass_utils import run_bass_kernel_spmd

    nc = bacc.Bacc("TRN2", target_bir_lowering=False, num_devices=1)
    biases = [np.asarray(v).reshape(D, 1) for v in (L0_attn_bq, L0_attn_bk, L0_attn_bv)]
    weights = [np.asarray(w) for w in (L0_attn_Wq, L0_attn_Wk, L0_attn_Wv, L0_attn_Wo, L0_ffn_Wg)]
    arrays = {
        "x": np.ascontiguousarray(L0_attn_x),
        "w_proj": np.ascontiguousarray(np.concatenate(weights + biases, axis=1)),
        "b_rows": np.concatenate([np.asarray(L0_attn_bo), np.asarray(L0_ffn_bg)]),
        "W1": np.ascontiguousarray(L0_ffn_W1),
        "W2": np.ascontiguousarray(L0_ffn_W2),
        "W3": np.ascontiguousarray(L0_ffn_W3),
    }
    arrays.update(constants())
    args = [nc.dram_tensor(name, a.shape, mybir.dt.from_np(a.dtype), kind="ExternalInput").ap()
            for name, a in arrays.items()]
    out = nc.dram_tensor("out", [B, S, D], F32, kind="ExternalOutput").ap()
    layer_kernel(nc, *args, out)
    results = run_bass_kernel_spmd(nc, [arrays], core_ids=[0])
    return results.results[0]["out"]
```
